# Optimizing a Trainium2 kernel written in Bass

```python
import numpy as np
import jax
import jax.numpy as jnp

def _softmax(x, axis=-1):
    return jax.nn.softmax(x, axis=axis)

def _gelu(x):
    return jax.nn.gelu(x, approximate=True)

def _silu(x):
    return jax.nn.silu(x)

def _sigmoid(x):
    return jax.nn.sigmoid(x)

def _layernorm(x, axis=-1, eps=1e-05):
    m = jnp.mean(x, axis=axis, keepdims=True)
    v = jnp.var(x, axis=axis, keepdims=True)
    return (x - m) / jnp.sqrt(v + eps)

def _scatter_add(tgt, idx, src, axis=0):
    return tgt.at[idx].add(src)

def _segment_sum(src, seg, n):
    return jax.ops.segment_sum(src, seg, n)
kernel_name = 'mk_decoder_postln_d1_seqx_r8_390068'

def setup_inputs(seed: int=0):
    np.random.seed(seed)
    _w = jnp.asarray

    def _rec_inputs():
        import jax
        import jax.numpy as jnp
        _rk = jax.random.key(seed)
        x = -0.0002928 + 1 * jax.random.normal(jax.random.fold_in(_rk, 1), (4, 256, 128), jnp.float32)
        _lenS = 256 - jax.random.randint(jax.random.fold_in(_rk, 7), (4,), 0, max(1, 256 // 4) + 1, jnp.int32)
        _lenS2 = 256 - jax.random.randint(jax.random.fold_in(_rk, 8), (4,), 0, max(1, 256 // 4) + 1, jnp.int32)
        _ctx_1024P = jax.random.normal(jax.random.fold_in(_rk, 11), (4, 16, 128), jnp.float32)
        _ctx_1024c = jax.random.dirichlet(jax.random.fold_in(_rk, 511), 0.3 * jnp.ones((16,), jnp.float32), (4, 256))
        _ctx_1024t = jnp.einsum('bsk,bkd->bsd', _ctx_1024c, _ctx_1024P)
        _ctx_1024t = _ctx_1024t * jax.lax.rsqrt(jnp.mean(jnp.square(_ctx_1024t)) + 1e-12) * 0.953939
        ctx_1024 = -1.39393e-06 + 0.999914 * (_ctx_1024t + 0.3 * jax.random.normal(jax.random.fold_in(_rk, 611), (4, 256, 128), jnp.float32))
        return (x, ctx_1024)
    x, ctx_1024 = _rec_inputs()

    def _L0_attn_setup():
        import jax, jax.numpy as jnp
        import numpy as np
        B, N, C, H = (2, 256, 128, 16)
        D = C // H
        EPS = 1e-12

        def l2norm(t):
            n = jnp.linalg.norm(t, axis=-1, keepdims=True)
            return t / jnp.maximum(n, EPS)
        key = jax.random.key(seed)
        k1, k2, k3 = jax.random.split(key, 3)
        x = jax.random.normal(k1, (B, N, C), dtype=jnp.float32)
        qkv_w = jax.random.normal(k2, (3 * C, C), dtype=jnp.float32) * (1.0 / np.sqrt(C))
        temperature = jnp.ones((H, 1, 1), dtype=jnp.float32)
        proj_w = jax.random.normal(k3, (C, C), dtype=jnp.float32) * (1.0 / np.sqrt(C))
        proj_b = jnp.zeros((C,), dtype=jnp.float32)
        return {'x': x, 'qkv_w': qkv_w, 'temperature': temperature, 'proj_w': proj_w, 'proj_b': proj_b}
    _L0_attn_all = _L0_attn_setup()
    _L0_attn_in = {k: v for k, v in _L0_attn_all.items() if k in ('qkv_w', 'temperature', 'proj_w', 'proj_b')}
    del _L0_attn_all

    def _L0_xattn_setup():
        import jax, jax.numpy as jnp
        import numpy as np
        import math
        D_MODEL = 128
        NUM_HEADS = 16
        MAX_LEN = 256
        D_HEAD = D_MODEL // NUM_HEADS
        BATCH = 2
        SEQ = 256

        def _skew(QEr):
            B, H, R, C = QEr.shape
            padded = jnp.pad(QEr, ((0, 0), (0, 0), (0, 0), (1, 0)))
            reshaped = padded.reshape(B, H, C + 1, R)
            return reshaped[:, :, 1:, :]
        root = jax.random.key(seed)
        ks = jax.random.split(root, 10)
        s = 1.0 / math.sqrt(D_MODEL)
        return {'query': jax.random.normal(ks[0], (BATCH, SEQ, D_MODEL), jnp.float32), 'key': jax.random.normal(ks[1], (BATCH, SEQ, D_MODEL), jnp.float32), 'value': jax.random.normal(ks[2], (BATCH, SEQ, D_MODEL), jnp.float32), 'Wq': jax.random.normal(ks[3], (D_MODEL, D_MODEL), jnp.float32) * s, 'bq': jax.random.normal(ks[4], (D_MODEL,), jnp.float32) * s, 'Wk': jax.random.normal(ks[5], (D_MODEL, D_MODEL), jnp.float32) * s, 'bk': jax.random.normal(ks[6], (D_MODEL,), jnp.float32) * s, 'Wv': jax.random.normal(ks[7], (D_MODEL, D_MODEL), jnp.float32) * s, 'bv': jax.random.normal(ks[8], (D_MODEL,), jnp.float32) * s, 'Er': jax.random.normal(ks[9], (MAX_LEN, D_HEAD), jnp.float32)}
    _L0_xattn_all = _L0_xattn_setup()
    _L0_xattn_in = {k: v for k, v in _L0_xattn_all.items() if k in ('Wq', 'bq', 'Wk', 'bk', 'Wv', 'bv', 'Er')}
    del _L0_xattn_all

    def _L0_ffn_setup():
        import jax, jax.numpy as jnp
        import numpy as np
        DIM = 128
        HIDDEN = 512
        E = 8
        B, S = (2, 512)
        key = jax.random.key(seed)
        ks = jax.random.split(key, 8)
        sd = 1.0 / np.sqrt(DIM)
        sh = 1.0 / np.sqrt(HIDDEN)
        return {'x': jax.random.normal(ks[0], (B, S, DIM), dtype=jnp.float32), 'router_w': jax.random.uniform(ks[1], (DIM, E), jnp.float32, -sd, sd), 'router_b': jax.random.uniform(ks[2], (E,), jnp.float32, -sd, sd), 'w1': jax.random.uniform(ks[3], (E, DIM, 2 * HIDDEN), jnp.float32, -sd, sd), 'b1': jax.random.uniform(ks[4], (E, 2 * HIDDEN), jnp.float32, -sd, sd), 'w2': jax.random.uniform(ks[5], (E, HIDDEN, DIM), jnp.float32, -sh, sh), 'b2': jax.random.uniform(ks[6], (E, DIM), jnp.float32, -sh, sh)}
    _L0_ffn_all = _L0_ffn_setup()
    _L0_ffn_in = {k: v for k, v in _L0_ffn_all.items() if k in ('router_w', 'router_b', 'w1', 'b1', 'w2', 'b2')}
    del _L0_ffn_all
    return {'x': x, 'ctx_1024': ctx_1024, 'L0_attn_qkv_w': _L0_attn_in['qkv_w'], 'L0_attn_temperature': _L0_attn_in['temperature'], 'L0_attn_proj_w': _L0_attn_in['proj_w'], 'L0_attn_proj_b': _L0_attn_in['proj_b'], 'L0_xattn_Wq': _L0_xattn_in['Wq'], 'L0_xattn_bq': _L0_xattn_in['bq'], 'L0_xattn_Wk': _L0_xattn_in['Wk'], 'L0_xattn_bk': _L0_xattn_in['bk'], 'L0_xattn_Wv': _L0_xattn_in['Wv'], 'L0_xattn_bv': _L0_xattn_in['bv'], 'L0_xattn_Er': _L0_xattn_in['Er'], 'L0_ffn_router_w': _L0_ffn_in['router_w'], 'L0_ffn_router_b': _L0_ffn_in['router_b'], 'L0_ffn_w1': _L0_ffn_in['w1'], 'L0_ffn_b1': _L0_ffn_in['b1'], 'L0_ffn_w2': _L0_ffn_in['w2'], 'L0_ffn_b2': _L0_ffn_in['b2']}

def reference(x, ctx_1024, L0_attn_qkv_w, L0_attn_temperature, L0_attn_proj_w, L0_attn_proj_b, L0_xattn_Wq, L0_xattn_bq, L0_xattn_Wk, L0_xattn_bk, L0_xattn_Wv, L0_xattn_bv, L0_xattn_Er, L0_ffn_router_w, L0_ffn_router_b, L0_ffn_w1, L0_ffn_b1, L0_ffn_w2, L0_ffn_b2):
    import jax
    import jax.numpy as jnp

    def _L0_attn_ref(x, qkv_w, temperature, proj_w, proj_b):
        import jax, jax.numpy as jnp
        import numpy as np
        B, N, C, H = (2, 256, 128, 16)
        D = C // H
        EPS = 1e-12

        def l2norm(t):
            n = jnp.linalg.norm(t, axis=-1, keepdims=True)
            return t / jnp.maximum(n, EPS)
        b, n, c = x.shape
        qkv = jnp.einsum('bnc,fc->bnf', x, qkv_w)
        q, k, v = jnp.split(qkv, 3, axis=-1)
        q = l2norm(q)
        k = l2norm(k)
        q = q.reshape(b, n, H, D).transpose(0, 2, 1, 3)
        k = k.reshape(b, n, H, D).transpose(0, 2, 1, 3)
        v = v.reshape(b, n, H, D).transpose(0, 2, 1, 3)
        scale = 1.0 / np.sqrt(D)
        q = q * scale
        k = k * scale
        attn = jnp.einsum('bhnd,bhkd->bhnk', q, k)
        attn = attn / temperature
        attn = jax.nn.softmax(attn, axis=-1)
        out = jnp.einsum('bhnk,bhkd->bhnd', attn, v)
        out = out.transpose(0, 2, 1, 3).reshape(b, n, c)
        out = jnp.einsum('bnc,oc->bno', out, proj_w) + proj_b
        return out

    def _L0_xattn_ref(query, key, value, Wq, bq, Wk, bk, Wv, bv, Er):
        import jax, jax.numpy as jnp
        import numpy as np
        import math
        D_MODEL = 128
        NUM_HEADS = 16
        MAX_LEN = 256
        D_HEAD = D_MODEL // NUM_HEADS
        BATCH = 2
        SEQ = 256

        def _skew(QEr):
            B, H, R, C = QEr.shape
            padded = jnp.pad(QEr, ((0, 0), (0, 0), (0, 0), (1, 0)))
            reshaped = padded.reshape(B, H, C + 1, R)
            return reshaped[:, :, 1:, :]
        B, S, D = query.shape
        H, dh = (NUM_HEADS, D_HEAD)
        q = (jnp.einsum('bsd,ed->bse', query, Wq) + bq).reshape(B, S, H, dh).transpose(0, 2, 1, 3)
        k = (jnp.einsum('bsd,ed->bse', key, Wk) + bk).reshape(B, S, H, dh).transpose(0, 2, 1, 3)
        v = (jnp.einsum('bsd,ed->bse', value, Wv) + bv).reshape(B, S, H, dh).transpose(0, 2, 1, 3)
        start = MAX_LEN - S
        Er_s = Er[start:, :]
        QEr = jnp.einsum('bhsd,ld->bhsl', q, Er_s)
        Srel = _skew(QEr)
        QK = jnp.einsum('bhsd,bhtd->bhst', q, k)
        attn = (QK + Srel) / math.sqrt(dh)
        causal = jnp.tril(jnp.ones((S, S), dtype=bool))
        attn = jnp.where(causal[None, None], attn, -jnp.inf)
        attn = jax.nn.softmax(attn, axis=-1)
        out = jnp.einsum('bhst,bhtd->bhsd', attn, v)
        out = out.transpose(0, 2, 1, 3).reshape(B, S, D)
        return out

    def _L0_ffn_ref(x, router_w, router_b, w1, b1, w2, b2):
        import jax, jax.numpy as jnp
        import numpy as np
        DIM = 128
        HIDDEN = 512
        E = 8
        B, S = (2, 512)
        logits = jnp.einsum('bsd,de->bse', x, router_w) + router_b
        probs = jax.nn.softmax(logits, axis=-1)
        top1 = jnp.argmax(probs, axis=-1)
        out = jnp.zeros_like(x)
        for i in range(E):
            h = jnp.einsum('bsd,df->bsf', x, w1[i]) + b1[i]
            a, g = jnp.split(h, 2, axis=-1)
            y = jnp.einsum('bsh,hd->bsd', a * jax.nn.sigmoid(g), w2[i]) + b2[i]
            out = out + jnp.where((top1 == i)[..., None], y, 0.0)
        return out
    x = _layernorm(x + _L0_attn_ref(x, L0_attn_qkv_w, L0_attn_temperature, L0_attn_proj_w, L0_attn_proj_b), axis=-1)
    x = _layernorm(x + _L0_xattn_ref(x, ctx_1024, ctx_1024, L0_xattn_Wq, L0_xattn_bq, L0_xattn_Wk, L0_xattn_bk, L0_xattn_Wv, L0_xattn_bv, L0_xattn_Er), axis=-1)
    x = _layernorm(x + _L0_ffn_ref(x, L0_ffn_router_w, L0_ffn_router_b, L0_ffn_w1, L0_ffn_b1, L0_ffn_w2, L0_ffn_b2), axis=-1)
    return x

_drawn_inputs = setup_inputs


def setup_inputs(seed=0):
    import zlib

    import numpy as np

    out = dict(_drawn_inputs(seed))
    spreads = {'L0_attn_temperature': (1.0, 0.6), 'L0_attn_proj_b': (0.0, 0.1)}
    factors = {'L0_xattn_bk': 8.0, 'L0_ffn_b1': 3.694}
    for name, (base, spread) in spreads.items():
        noise = np.random.default_rng([zlib.crc32(name.encode()), seed]).standard_normal(out[name].shape)
        drawn = base * np.exp(spread * noise) if base else spread * noise
        out[name] = jnp.asarray(drawn.astype(out[name].dtype))
    for name, factor in factors.items():
        out[name] = (out[name] * factor).astype(out[name].dtype)
    return out
```

```python
from contextlib import ExitStack

import concourse.bass as bass
from concourse import mybir

FP32 = mybir.dt.float32
BF16 = mybir.dt.bfloat16
I32 = mybir.dt.int32
ALU = mybir.AluOpType
ACT = mybir.ActivationFunctionType
AX = mybir.AxisListType

NB, NT, C = 4, 256, 128
H, D = 16, 8
P = 128
TT = NT // P
HEADS_A_GROUP = 4
NG = H // HEADS_A_GROUP
VW = 32
NTERM = 6
SR = NTERM * D
QB = 32
NQB = NT // QB
E, F = 8, 512
SLOTS = P
NTILE = NB * TT + E - 1
LN_EPS = 1e-5
MASKED = -1e30

A_BOX = ("qkv0", "qkv1", "qkT", "shiftT", "pv0", "norm0", "pv1", "norm1", "oT", "proj", "x1T", "q2T")
B_BOX = ("kv", "tr0", "tr1", "tr2", "tr3", "pv0", "norm0",
         "tr4", "tr5", "tr6", "tr7", "pv1", "norm1", "x2T", "logits")


def build(nc, x_rows, x_cols, ctx_cols, wqkv_t, temperature, wproj_t, proj_b, wq_t, bq, wk_t, bk, wv_t, bv,
          er_t, router_w, router_b, w1, b1, w2, b2, out):
    ctx = ExitStack()
    with ctx:
        def sb(name, shape, dt=FP32):
            return ctx.enter_context(nc.sbuf_tensor(name, shape, dt))

        def pb(name, shape, dt=FP32):
            return ctx.enter_context(nc.psum_tensor(name, shape, dt))

        def sem(name):
            return ctx.enter_context(nc.semaphore(name))

        def dram(name, shape, dt=FP32):
            return nc.dram_tensor(name, shape, dt, kind="Internal").ap()

        parts_a = dram("parts_a", (NB, 2, NTERM, P, NT), BF16)
        parts_b = dram("parts_b", (NB, 2, NTERM, P, NT), BF16)
        shift_a = dram("shift_a", (NB, TT, H, P), BF16)
        sorted_x = dram("sorted_x", (NTILE * SLOTS, C))
        sorted_y = dram("sorted_y", (NTILE * SLOTS, C))

        ident = sb("ident", [P, P])
        identb = sb("identb", [P, P], BF16)
        ones_b = sb("ones_b", [P, P], BF16)
        before = sb("before", [P, P], BF16)
        parity = sb("parity", [P, NT], BF16)
        pad = sb("pad", [P, 1])
        half = sb("half", [P, 4])
        wqkv = sb("wqkv", [P, 3 * C])
        wproj = sb("wproj", [P, C])
        wq = sb("wq", [P, C])
        wk = sb("wk", [P, C])
        wv = sb("wv", [P, C])
        wr = sb("wr", [P, E])
        pbias = sb("pbias", [P, C])
        bv_row = sb("bv_row", [P, C])
        rb_row = sb("rb_row", [P, E])
        bq_col = sb("bq_col", [P, 1])
        bk_col = sb("bk_col", [P, 1])
        temp = sb("temp", [P, H])
        trow = sb("trow", [P, D, H])
        er_parts = sb("er_parts", [D, 3, NT], BF16)
        er_mask = sb("er_mask", [1, 2 * NT], BF16)
        EW = 400
        ErS = sb("ErS", [P, EW], BF16)
        w1_sb = sb("w1_sb", [P, E, 2 * F])
        w2_sb = sb("w2_sb", [P, E, F // P, C])

        xT = sb("xT", [P, NT])
        x_tok = sb("x_tok", [P, TT, C])
        xpb = sb("xpb", [P, TT, C])
        qkv = sb("qkv", [P, TT, 3 * C])
        sq = sb("sq", [P, 4, C])
        n2 = sb("n2", [P, 4])
        n2c = sb("n2c", [P, 4])
        rn = sb("rn", [P, 4])
        qkn = sb("qkn", [P, TT, 2, D, H])
        qkT = sb("qkT", [P, 2, NT])
        restA = sb("restA", [P, 2, NT])
        SpA = sb("SpA", [P, 3, 2, NT], BF16)
        V1 = sb("V1", [P, TT, H, VW])
        QS = sb("QS", [P, H, NT], BF16)
        KS = sb("KS", [P, H, NT], BF16)
        negm1 = sb("negm1", [P, TT, H], BF16)
        nmT = sb("nmT", [TT * H, P], BF16)
        P1 = sb("P1", [P, 2, TT, HEADS_A_GROUP, NT])
        OT1 = sb("OT1", [P, 2 * NT])
        rden1 = sb("rden1", [P, TT, 2 * HEADS_A_GROUP])
        O1 = sb("O1", [P, TT, C])
        O1T = sb("O1T", [P, NT])
        res1 = sb("res1", [P, TT, C])
        st1 = sb("st1", [P, TT, 6])
        mv1 = sb("mv1", [P, TT, 2])
        ve1 = sb("ve1", [P, TT])
        rs1 = sb("rs1", [P, TT])
        x1 = sb("x1", [P, TT, C])
        x1T = sb("x1T", [P, NT])

        cT = sb("cT", [P, NT])
        qk2T = sb("qk2T", [P, 2, NT])
        restB = sb("restB", [P, 2, NT])
        SpB = sb("SpB", [P, 3, 2, NT], BF16)
        V2 = sb("V2", [P, TT, H, VW])
        QZ = sb("QZ", [P, H, NT], BF16)
        KZ = sb("KZ", [P, H, NT], BF16)
        Z = sb("Z", [P, H, NT], BF16)
        KS2 = sb("KS2", [P, H, NT], BF16)
        Sb = sb("Sb", [P, 2, 512], BF16)
        Sm = sb("Sm", [P, 2, 512], BF16)
        negm2 = sb("negm2", [P, NQB, 4], BF16)
        P2a = sb("P2a", [P, H, P])
        P2b = sb("P2b", [P, 2, H, P])
        er = P2a[0:D, 0:2, :].rearrange("d h q -> d (h q)")
        er_rest = P2a[0:D, 2:4, :].rearrange("d h q -> d (h q)")
        OT2 = sb("OT2", [P, 512])
        rden2 = sb("rden2", [P, H])
        O2 = sb("O2", [P, TT, C])
        res2 = sb("res2", [P, TT, C])
        st2 = sb("st2", [P, TT, 6])
        mv2 = sb("mv2", [P, TT, 2])
        ve2 = sb("ve2", [P, TT])
        rs2 = sb("rs2", [P, TT])
        x2 = sb("x2", [P, TT, C])
        x2T = sb("x2T", [P, NT])
        x2all = sb("x2all", [P, NB * TT, C])
        logits = sb("logits", [P, NB * TT, E])

        NTK = NB * TT
        iota_e = sb("iota_e", [P, E])
        iota_t = sb("iota_t", [P, NTILE])
        iota_c = sb("iota_c", [P, NTK])
        mx = sb("mx", [P, NTK])
        eq = sb("eq", [P, NTK, E])
        cand = sb("cand", [P, NTK, E])
        first = sb("first", [P, NTK])
        oh = sb("oh", [P, NTK, E])
        ohb = sb("ohb", [P, NTK, E], BF16)
        cnt = sb("cnt", [P, E])
        gt = sb("gt", [P, E, NTK])
        nti = sb("nti", [P, E])
        ends = sb("ends", [P, E])
        base = sb("base", [P, E])
        pos = sb("pos", [P, NTK, E])
        slotf = sb("slotf", [P, NTK])
        slot = sb("slot", [P, NTK], I32)
        le = sb("le", [P, NTILE, E])
        tef = sb("tef", [P, NTILE])
        tile_e = sb("tile_e", [P, NTILE], I32)

        zrow = sb("zrow", [P, C])
        xg = sb("xg", [P, C])
        xgT = sb("xgT", [P, P])
        b2t = sb("b2t", [P, C])
        y = sb("y", [P, C])
        room1 = P1[:, :, :, :, :].rearrange("p g k h q -> p (g k h q)")
        aa, gs, sg, act_, actT = (room1[:, k * F:(k + 1) * F] for k in range(5))
        b1t = room1[:, 5 * F:7 * F]
        room2 = P2b[:, :, :, :].rearrange("p k h q -> p (k h q)")
        yg, res3, x3 = (room2[:, k * NTK * C:(k + 1) * NTK * C].rearrange("p (t c) -> p t c", c=C) for k in range(3))
        st3 = sb("st3", [P, NTK, 6])
        mv3 = sb("mv3", [P, NTK, 2])
        ve3 = sb("ve3", [P, NTK])
        rs3 = sb("rs3", [P, NTK])

        SA = pb("SA", [P, 2, 512])
        MA = pb("MA", [P, 512])
        SB = pb("SB", [P, 4, 512])
        MB = pb("MB", [P, 512])
        MAb = MA[:, :].bitcast(BF16)
        MBb = MB[:, :].bitcast(BF16)

        s = {n: sem(n) for n in (
            "w_in", "c_in", "er_in", "fill", "consts", "erdone", "er_stacked", "zero_out", "bigw",
            "xT_in", "xtok_in", "ma_full", "ma_free", "n2_ok", "n2c_ok", "rn_ok", "qkn_ok", "qkT_ok", "v1_ok",
            "xpb_ok", "spa_ok", "pa_out", "qs_in", "sa_full", "sa_free", "negm1_ok", "nmT_ok", "m_out", "m_in",
            "st_full", "exp1", "pv1_done", "ot1_ok", "o1_ok", "o1T_ok", "ve1_ok", "rs1_ok", "x1_ok", "x1T_ok",
            "res1_ok",
            "cT_in", "mb_full", "mb_free", "k2_ok", "q2_ok", "v2_ok", "spb_ok", "pb_out", "qz_in", "z_ok",
            "sc_full", "copied", "maxed", "negm2_ok", "shifted", "exp2", "pv2_done", "ot2_ok", "o2_ok",
            "ve2_ok", "rs2_ok", "x2_ok", "x2T_ok", "x2all_ok", "lg_ok",
            "r_a", "r_full", "slot_ok", "te_ok", "scat", "xg_in", "xgT_full", "xgT_ok", "up_full", "aa_ok", "gs_ok", "sg_ok",
            "act_ok", "actT_full", "actT_ok", "down_full", "y_ok", "y_out", "bt_in", "gath", "ve3_ok", "rs3_ok",
            "x3_ok", "o_out", "dchain", "pchain", "achain",
        )}
        block = ctx.enter_context(nc.Block())

        def a_full(b, use):
            return b * len(A_BOX) + A_BOX.index(use) + 1

        def b_full(b, use):
            return b * len(B_BOX) + B_BOX.index(use) + 1

        def one(ap):
            return ap.squeeze(0)

        @block.sync
        def _(sp):
            def load(dst, src, name):
                sp.dma_start(dst, src).then_inc(s[name], 16)

            load(wqkv[:, :], wqkv_t, "w_in")
            load(temp[:, :], temperature.partition_broadcast(P), "c_in")
            load(pbias[:, :], proj_b.partition_broadcast(P), "c_in")
            load(wproj[:, :], wproj_t, "w_in")
            load(wq[:, :], wq_t, "w_in")
            load(wk[:, :], wk_t, "w_in")
            load(wv[:, :], wv_t, "w_in")
            load(wr[:, :], router_w, "w_in")
            load(bv_row[:, :], bv.partition_broadcast(P), "c_in")
            load(rb_row[:, :], router_b.partition_broadcast(P), "c_in")
            load(bq_col[:, :], bq.unsqueeze(1), "c_in")
            load(bk_col[:, :], bk.unsqueeze(1), "c_in")
            load(er[:, :], er_t, "er_in")
            sp.wait_ge(s["erdone"], 1)
            sp.wait_ge(s["fill"], 1)
            for half_, at in ((0, 0), (64, 1)):
                for blk, w in enumerate((0, 0, 0, 1, 1, 2)):
                    load(ErS[half_ + D * blk:half_ + D * blk + D, at:at + NT], er_parts[:, w, :], "er_stacked")
                load(ErS[half_ + SR:half_ + SR + 1, NT + at:NT + at + 140], er_mask[:, NT:NT + 140], "er_stacked")
            with sp.Fori(0, NB) as b:
                sp.wait_ge(s["ma_full"], b * len(A_BOX))
                load(xT[:, :], one(x_cols[bass.ds(b, 1), :, :]), "xT_in")
                sp.wait_ge(s["xpb_ok"], b)
                load(x_tok[:, :, :], one(x_rows[bass.ds(b, 1), :, :, :]), "xtok_in")
                sp.wait_ge(s["mb_full"], b * len(B_BOX))
                load(cT[:, :], one(ctx_cols[bass.ds(b, 1), :, :]), "cT_in")
                sp.wait_ge(s["spa_ok"], b + 1)
                for parts, Sp, name in ((parts_a, SpA, "pa_out"),):
                    pv = one(parts[bass.ds(b, 1), :, :, :, :])
                    load(pv[0, 0:3].rearrange("w p t -> p w t"), Sp[:, :, 0, :], name)
                    load(pv[0, 3:5].rearrange("w p t -> p w t"), Sp[:, 0:2, 0, :], name)
                    load(pv[0, 5], Sp[:, 0, 0, :], name)
                    load(pv[1, 0:3].rearrange("w p t -> p w t"), Sp[:, 0, 1, :].unsqueeze(1).broadcast_to([P, 3, NT]), name)
                    load(pv[1, 3:5].rearrange("w p t -> p w t"), Sp[:, 1, 1, :].unsqueeze(1).broadcast_to([P, 2, NT]), name)
                    load(pv[1, 5], Sp[:, 2, 1, :], name)
                sp.wait_ge(s["pa_out"], b * 96 + 96)
                pv = one(parts_a[bass.ds(b, 1), :, :, :, :])
                load(QS[0:SR, :, :], pv[0].rearrange("w (d h) t -> (w d) h t", h=H), "qs_in")
                load(KS[0:SR, :, :], pv[1].rearrange("w (d h) t -> (w d) h t", h=H), "qs_in")
                sp.wait_ge(s["nmT_ok"], b + 1)
                sh = one(shift_a[bass.ds(b, 1), :, :, :])
                load(sh.rearrange("q h t -> (q h) t"), nmT[:, :], "m_out")
                sp.wait_ge(s["m_out"], b * 16 + 16)
                load(QS[96:97, :, :].rearrange("o h (q t) -> o h q t", q=TT), sh.rearrange("q h t -> h q t").unsqueeze(0), "m_in")
                sp.wait_ge(s["spb_ok"], b + 1)
                pv = one(parts_b[bass.ds(b, 1), :, :, :, :])
                load(pv[0, 0:3].rearrange("w p t -> p w t"), SpB[:, :, 0, :], "pb_out")
                load(pv[0, 3:5].rearrange("w p t -> p w t"), SpB[:, 0:2, 0, :], "pb_out")
                load(pv[0, 5], SpB[:, 0, 0, :], "pb_out")
                load(pv[1, 0:3].rearrange("w p t -> p w t"), SpB[:, 0, 1, :].unsqueeze(1).broadcast_to([P, 3, NT]), "pb_out")
                load(pv[1, 3:5].rearrange("w p t -> p w t"), SpB[:, 1, 1, :].unsqueeze(1).broadcast_to([P, 2, NT]), "pb_out")
                load(pv[1, 5], SpB[:, 2, 1, :], "pb_out")
                sp.wait_ge(s["pb_out"], b * 96 + 96)
                for half_ in (0, 64):
                    load(QZ[half_:half_ + SR, :, :], pv[0].rearrange("w (d h) t -> (w d) h t", h=H), "qz_in")
                    load(KZ[half_:half_ + SR, :, :], pv[1].rearrange("w (d h) t -> (w d) h t", h=H), "qz_in")
            sp.wait_ge(s["te_ok"], 1)
            sp.wait_ge(s["scat"], 16 * NTK)
            with sp.Fori(0, NTILE) as j:
                e = sp.value_load(tile_e[0:1, bass.ds(j, 1)], min_val=0, max_val=E - 1)
                sp.wait_ge(s["xgT_full"], j)
                load(xg[:, :], sorted_x[bass.ds(j * SLOTS, SLOTS), :], "xg_in")
                sp.wait_ge(s["y_ok"], j)
                load(b1t[:, :], one(b1[bass.ds(e, 1), :]).partition_broadcast(P), "bt_in")
                load(b2t[:, :], one(b2[bass.ds(e, 1), :]).partition_broadcast(P), "bt_in")
                sp.wait_ge(s["y_ok"], j + 1)
                load(sorted_y[bass.ds(j * SLOTS, SLOTS), :], y[:, :], "y_out")
            sp.wait_ge(s["x3_ok"], 1)
            load(out.rearrange("b (t p) c -> p (b t) c", p=P), x3[:, :, :], "o_out")
            sp.wait_ge(s["o_out"], 16)

        @block.gpsimd
        def _(pool):
            n = [0]

            def link(ins):
                ins.then_inc(s["pchain"], 1)
                n[0] += 1
                pool.wait_ge(s["pchain"], n[0])

            g = nc.gpsimd
            link(g.memset(ident[:, :], 0.0))
            link(g.affine_select(out=ident[:, :], in_=ident[:, :], compare_op=ALU.not_equal, fill=1.0,
                                 base=0, pattern=[[-1, P]], channel_multiplier=1))
            link(g.memset(half[:, :], -0.5))
            link(g.memset(before[:, :], 1.0))
            link(g.affine_select(out=before[:, :], in_=before[:, :], compare_op=ALU.is_gt, fill=0.0,
                                 base=0, pattern=[[1, P]], channel_multiplier=-1))
            link(g.iota(iota_e[:, :], pattern=[[1, E]], base=-E, channel_multiplier=0, allow_small_or_imprecise_dtypes=True))
            link(g.iota(iota_t[:, :], pattern=[[1, NTILE]], base=0, channel_multiplier=0, allow_small_or_imprecise_dtypes=True))
            link(g.iota(iota_c[:, :], pattern=[[SLOTS, NTK]], base=0, channel_multiplier=0, allow_small_or_imprecise_dtypes=True))
            g.tensor_copy(identb[:, :], ident[:, :]).then_inc(s["consts"], 1)
            pool.dma_start(w1_sb[:, :, :], w1.rearrange("e c f -> c e f")).then_inc(s["bigw"], 16)
            pool.dma_start(w2_sb[:, :, :, :], w2.rearrange("e (k f) c -> f e k c", f=P)).then_inc(s["bigw"], 16)
            pool.wait_ge(s["fill"], 1)
            pool.dma_start(sorted_x.rearrange("(j p) c -> p j c", p=P),
                           zrow[:, :].unsqueeze(1).broadcast_to([P, NTILE, C])).then_inc(s["zero_out"], 16)
            with pool.Fori(0, NB) as b:
                pool.wait_ge(s["n2c_ok"], b + 1)
                g.tensor_tensor(out=rn[:, :], in0=n2c[:, :], in1=half[:, :], op=ALU.pow).then_inc(s["rn_ok"], 1)
                pool.wait_ge(s["xtok_in"], b * 16 + 16)
                pool.wait_ge(s["c_in"], 16 * 6)
                pool.wait_ge(s["res1_ok"], b)
                g.tensor_tensor(out=xpb[:, :, :], in0=x_tok[:, :, :],
                                in1=pbias[:, :].unsqueeze(1).broadcast_to([P, TT, C]), op=ALU.add).then_inc(s["xpb_ok"], 1)
                pool.wait_ge(s["ve1_ok"], b + 1)
                g.tensor_tensor(out=rs1[:, :], in0=ve1[:, :], in1=half[:, 0:TT], op=ALU.pow).then_inc(s["rs1_ok"], 1)
                pool.wait_ge(s["ve2_ok"], b + 1)
                g.tensor_tensor(out=rs2[:, :], in0=ve2[:, :], in1=half[:, 0:TT], op=ALU.pow).then_inc(s["rs2_ok"], 1)
            pool.wait_ge(s["slot_ok"], 1)
            pool.wait_ge(s["zero_out"], 16)
            pool.wait_ge(s["x2all_ok"], NB)
            for t in range(NTK):
                pool.indirect_dma_start(out=sorted_x, out_offset=bass.IndirectOffsetOnAxis(ap=slot[:, t:t + 1], axis=0),
                                        in_=x2all[:, t, :], in_offset=None).then_inc(s["scat"], 16)
            pool.wait_ge(s["y_out"], 16 * NTILE)
            for t in range(NTK):
                pool.indirect_dma_start(out=yg[:, t, :], out_offset=None, in_=sorted_y,
                                        in_offset=bass.IndirectOffsetOnAxis(ap=slot[:, t:t + 1], axis=0)).then_inc(s["gath"], 16)
            pool.wait_ge(s["ve3_ok"], 1)
            g.tensor_tensor(out=rs3[:, :], in0=ve3[:, :], in1=half[:, 0:1].broadcast_to([P, NTK]), op=ALU.pow).then_inc(s["rs3_ok"], 1)

        @block.scalar
        def _(act):
            a = nc.scalar

            def copy(dst, src):
                return a.activation(dst, src, ACT.Copy)

            with act.Fori(0, NB) as b:
                for t in range(TT):
                    act.wait_ge(s["ma_full"], a_full(b, f"qkv{t}"))
                    if t == 0:
                        act.wait_ge(s["qkn_ok"], b)
                        act.wait_ge(s["v1_ok"], b)
                    copy(qkv[:, t, :], MA[:, 0:3 * C]).then_inc(s["ma_free"], 1)
                act.wait_ge(s["ma_free"], a_full(b, "qkv1"))
                for t in range(TT):
                    for k in range(2):
                        ins = a.activation(sq[:, 2 * t + k, :], qkv[:, t, k * C:(k + 1) * C], ACT.Square,
                                           accum_out=n2[:, 2 * t + k:2 * t + k + 1])
                ins.then_inc(s["n2_ok"], 1)
                act.wait_ge(s["pv1_done"], b * NG)
                a.activation(V1[:, :, :, 0:D], qkv[:, :, 2 * C:3 * C].rearrange("p t (h d) -> p t h d", d=D), ACT.Copy)\
                    .then_inc(s["v1_ok"], 1)
                act.wait_ge(s["ma_full"], a_full(b, "qkT"))
                act.wait_ge(s["spa_ok"], b)
                copy(qkT[:, :, :], MA[:, :].rearrange("p (w t) -> p w t", w=2)).then_inc(s["ma_free"], 1)
                act.wait_ge(s["ma_full"], a_full(b, "shiftT"))
                act.wait_ge(s["m_out"], b * 16)
                copy(nmT[:, :], MAb[0:TT * H, 0:P]).then_inc(s["nmT_ok"], 1)
                act.wait_ge(s["nmT_ok"], b + 1)
                act.sem_inc(s["ma_free"], 1)
                for grp in range(NG):
                    for i in range(2):
                        u = 2 * grp + i
                        act.wait_ge(s["st_full"], b * 8 + u + 1)
                        act.wait_ge(s["pv1_done"], b * NG + max(grp - 1, 0))
                        a.activation(P1[:, grp % 2, :, 2 * i:2 * i + 2, :].rearrange("p k h t -> p k (h t)"),
                                     SA[:, :, :], ACT.Exp).then_inc(s["exp1"], 1)
                    if grp % 2:
                        act.wait_ge(s["ma_full"], a_full(b, f"pv{grp // 2}"))
                        if grp == 3:
                            act.wait_ge(s["ma_full"], a_full(b, "norm0"))
                        copy(OT1[:, :], MA[:, :]).then_inc(s["ma_free"], 1)
                act.wait_ge(s["ma_full"], a_full(b, "oT"))
                copy(O1T[:, :], MA[:, 0:NT]).then_inc(s["ma_free"], 1)
                act.wait_ge(s["ma_full"], a_full(b, "x1T"))
                copy(x1T[:, :], MA[:, 0:NT]).then_inc(s["ma_free"], 1)
                for qb in range(NQB):
                    slot_ = qb % 2
                    act.wait_ge(s["sc_full"], b * NQB + qb + 1)
                    act.wait_ge(s["mb_full"], b_full(b, f"tr{qb - 2}") if qb >= 2 else b * len(B_BOX))
                    if qb >= 6:
                        act.wait_ge(s["maxed"], b * 4 + qb - 5)
                    copy(Sb[:, slot_, :], SB[:, 2 * slot_, :]).then_inc(s["copied"], 1)
                    act.wait_ge(s["shifted"], b * NQB + qb + 1)
                    act.wait_ge(s["pv2_done"], b * TT)
                    qs = slice(QB * (qb % 4), QB * (qb % 4) + QB)
                    if qb < 4:
                        a.activation(P2a[:, :, qs], SB[:, 2 * slot_, :].rearrange("p (h q) -> p h q", h=H),
                                     ACT.Exp).then_inc(s["exp2"], 1)
                    else:
                        a.activation(P2b[:, :, :, qs].rearrange("p k h q -> p (k h) q"),
                                     SB[:, 2 * slot_:2 * slot_ + 2, :].rearrange("p k (h q) -> p (k h) q", h=H),
                                     ACT.Exp).then_inc(s["exp2"], 1)
                    if qb % 4 == 3:
                        qt = qb // 4
                        act.wait_ge(s["mb_full"], b_full(b, f"pv{qt}"))
                        copy(OT2[:, :], MB[:, :]).then_inc(s["mb_free"], 1)
                act.wait_ge(s["x2_ok"], b + 1)
                copy(x2all[:, bass.ds(b * TT, TT), :], x2[:, :, :]).then_inc(s["x2all_ok"], 1)
                act.wait_ge(s["mb_full"], b_full(b, "x2T"))
                copy(x2T[:, :], MB[:, 0:NT]).then_inc(s["mb_free"], 1)
            with act.Fori(0, NTILE) as j:
                act.wait_ge(s["xgT_full"], j + 1)
                act.wait_ge(s["up_full"], j)
                copy(xgT[:, :], MA[:, 0:P]).then_inc(s["xgT_ok"], 1)
                act.wait_ge(s["gs_ok"], j + 1)
                a.activation(sg[:, :], gs[:, :], ACT.Sigmoid).then_inc(s["sg_ok"], 1)
                act.wait_ge(s["actT_full"], j + 1)
                act.wait_ge(s["down_full"], j)
                copy(actT[:, :], MB[:, :]).then_inc(s["actT_ok"], 1)

        @block.vector
        def _(dve):
            v = nc.vector
            n = [0]
            turn = [0, 0]

            def link(ins):
                ins.then_inc(s["dchain"], 1)
                n[0] += 1
                dve.wait_ge(s["dchain"], turn[0] * turn[1] + n[0])

            link(v.memset(ErS[:, :], 0.0))
            link(v.memset(zrow[:, :], 0.0))
            for t_ in (QS, KS, QZ, KZ):
                link(v.memset(t_[:, :, :], 0.0))
            link(v.memset(er_mask[:, :], MASKED))
            link(v.memset(KS[96:97, :, :], 1.0))
            link(v.memset(QZ[32:64, :, :], 1.0))
            link(v.memset(QZ[96:128, :, :], 1.0))
            link(v.memset(parity[:, :], 0.0))
            link(v.memset(parity[0:64, 0:NT:2], 1.0))
            link(v.memset(parity[64:128, 1:NT:2], 1.0))
            link(v.memset(V1[:, :, :, :], 0.0))
            link(v.memset(V2[:, :, :, :], 0.0))
            link(v.memset(V1[:, :, :, D:D + 1], 1.0))
            link(v.memset(V2[:, :, :, D:D + 1], 1.0))
            v.memset(ones_b[:, :], 1.0).then_inc(s["fill"], 1)
            dve.wait_ge(s["er_in"], 16)
            link(v.tensor_copy(er_parts[:, 0, :], er[:, :]))
            link(v.tensor_tensor(out=er_rest[:, :], in0=er[:, :], in1=er_parts[:, 0, :], op=ALU.subtract))
            link(v.tensor_copy(er_parts[:, 1, :], er_rest[:, :]))
            v.tensor_tensor(out=er_parts[:, 2, :], in0=er_rest[:, :], in1=er_parts[:, 1, :], op=ALU.subtract)\
                .then_inc(s["erdone"], 1)
            dve.wait_ge(s["c_in"], 16 * 6)
            link(v.reciprocal(temp[:, :], temp[:, :]))
            link(v.tensor_scalar(trow[:, :, :], temp[:, :].unsqueeze(1).broadcast_to([P, D, H]), 1.0 / D, None, ALU.mult))

            def split(parts, whole, rest, ready):
                link(v.tensor_copy(parts[:, 0, :, :], whole))
                link(v.tensor_tensor(out=rest[:, :, :], in0=whole, in1=parts[:, 0, :, :], op=ALU.subtract))
                link(v.tensor_copy(parts[:, 1, :, :], rest[:, :, :]))
                v.tensor_tensor(out=parts[:, 2, :, :], in0=rest[:, :, :], in1=parts[:, 1, :, :],
                                op=ALU.subtract).then_inc(ready, 1)

            def layer_norm(b, r, st, mv, ve, rs, dst, ntiles, ve_ok, rs_ok, done):
                for t in range(ntiles):
                    link(v.bn_stats(st[:, t, :], r[:, t, :]))
                v.memset(pad[:, :], 0.0)
                for t in range(ntiles):
                    ins = v.bn_aggr(mv[:, t, :], st[:, t, :])
                link(ins)
                v.tensor_scalar(ve[:, :], mv[:, :, 1], LN_EPS, None, ALU.add).then_inc(ve_ok, 1)
                dve.wait_ge(rs_ok, b + 1)
                for t in range(ntiles):
                    ins = v.tensor_scalar(dst[:, t, :], r[:, t, :], mv[:, t, 0:1], rs[:, t:t + 1], ALU.subtract, ALU.mult)
                ins.then_inc(done, 1)

            def body(b):
                dve.wait_ge(s["n2_ok"], b + 1)
                v.tensor_scalar(n2c[:, :], n2[:, :], 1e-24, None, ALU.max).then_inc(s["n2c_ok"], 1)
                dve.wait_ge(s["rn_ok"], b + 1)
                for t in range(TT):
                    v.scalar_tensor_tensor(out=qkn[:, t, 0, :, :].rearrange("p d h -> p h d"),
                                           in0=qkv[:, t, 0:C].rearrange("p (h d) -> p h d", d=D),
                                           scalar=rn[:, 2 * t:2 * t + 1],
                                           in1=trow[:, :, :].rearrange("p d h -> p h d"), op0=ALU.mult, op1=ALU.mult)
                    ins = v.tensor_scalar(qkn[:, t, 1, :, :].rearrange("p d h -> p h d"),
                                          qkv[:, t, C:2 * C].rearrange("p (h d) -> p h d", d=D),
                                          rn[:, 2 * t + 1:2 * t + 2], None, ALU.mult)
                ins.then_inc(s["qkn_ok"], 1)
                dve.wait_ge(s["ma_free"], a_full(b, "qkT"))
                dve.wait_ge(s["pa_out"], b * 96)
                split(SpA, qkT[:, :, :], restA, s["spa_ok"])
                for u in range(16):
                    hp, qt = divmod(u, 2)
                    dve.wait_ge(s["sa_full"], b * 16 + u + 1)
                    v.tensor_reduce(out=negm1[:, qt, 2 * hp:2 * hp + 2], in_=SA[:, u % 2, :].rearrange("p (h k) -> p h k", h=2),
                                    axis=AX.X, op=ALU.max, negate=True).then_inc(s["negm1_ok"], 1)

                def normalise(box, rden, dst, groups):
                    link(v.reciprocal(rden, box[:, :, :, D]))
                    return v.tensor_tensor(out=dst, in0=box[:, :, :, 0:D], in1=rden.unsqueeze(3).broadcast_to([P, box.shape[1], box.shape[2], D]), op=ALU.mult)

                for pair in range(2):
                    dve.wait_ge(s["ma_full"], a_full(b, f"norm{pair}"))
                    normalise(MA[:, :].rearrange("p (q h w) -> p q h w", q=TT, w=VW), rden1[:, :, :],
                              O1[:, :, 64 * pair:64 * pair + 64].rearrange("p q (h d) -> p q h d", d=D), 2)\
                        .then_inc(s["o1_ok"], 1)
                    dve.wait_ge(s["o1_ok"], 2 * b + pair + 1)
                    dve.sem_inc(s["ma_free"], 1)
                dve.wait_ge(s["ma_full"], a_full(b, "proj"))
                dve.wait_ge(s["xpb_ok"], b + 1)
                v.tensor_tensor(out=res1[:, :, :], in0=MA[:, 0:NT].rearrange("p (t c) -> p t c", t=TT), in1=xpb[:, :, :],
                                op=ALU.add).then_inc(s["res1_ok"], 1)
                dve.wait_ge(s["res1_ok"], b + 1)
                dve.sem_inc(s["ma_free"], 1)
                layer_norm(b, res1, st1, mv1, ve1, rs1, x1, TT, s["ve1_ok"], s["rs1_ok"], s["x1_ok"])
                dve.wait_ge(s["mb_full"], b_full(b, "kv"))
                dve.wait_ge(s["spb_ok"], b)
                v.tensor_scalar(qk2T[:, 1, :], MB[:, 0:NT], bk_col[:, :], None, ALU.add)
                dve.wait_ge(s["pv2_done"], b * TT)
                link(v.tensor_tensor(out=V2[:, :, :, 0:D], in0=MB[:, NT:2 * NT].rearrange("p (t h d) -> p t h d", t=TT, d=D),
                                in1=bv_row[:, :].rearrange("p (h d) -> p h d", d=D).unsqueeze(1).broadcast_to([P, TT, H, D]),
                                op=ALU.add))
                dve.sem_inc(s["v2_ok"], 1)
                dve.sem_inc(s["mb_free"], 1)
                dve.wait_ge(s["ma_full"], a_full(b, "q2T"))
                v.tensor_scalar(qk2T[:, 0, :], MA[:, 0:NT], bq_col[:, :], float(D) ** -0.5, ALU.add, ALU.mult)\
                    .then_inc(s["q2_ok"], 1)
                dve.wait_ge(s["q2_ok"], b + 1)
                dve.sem_inc(s["ma_free"], 1)
                dve.wait_ge(s["pb_out"], b * 96)
                split(SpB, qk2T[:, :, :], restB, s["spb_ok"])
                dve.wait_ge(s["qz_in"], b * 64 + 64)
                dve.wait_ge(s["sc_full"], b * NQB)
                v.tensor_copy(KS2[:, :, :], KZ[:, :, :])
                v.tensor_tensor(out=Z[:, :, :], in0=QZ[:, :, :],
                                in1=parity[:, :].unsqueeze(1).broadcast_to([P, H, NT]), op=ALU.mult).then_inc(s["z_ok"], 1)
                for qb in range(NQB):
                    if qb >= 4:
                        dve.wait_ge(s["copied"], b * NQB + qb + 1)
                        v.tensor_tensor(out=Sm[:, qb % 2, :], in0=SB[:, 2 * (qb % 2) + 1, :], in1=Sb[:, qb % 2, :],
                                        op=ALU.max).then_inc(s["maxed"], 1)
                    dve.wait_ge(s["mb_full"], b_full(b, f"tr{qb}"))
                    v.tensor_reduce(out=negm2[:, qb, :], in_=MBb[:, 0:512].rearrange("p (c k) -> p c k", c=4), axis=AX.X,
                                    op=ALU.max, negate=True).then_inc(s["negm2_ok"], 1)
                    dve.wait_ge(s["negm2_ok"], b * NQB + qb + 1)
                    dve.sem_inc(s["mb_free"], 1)
                    if qb % 4 == 3:
                        qt = qb // 4
                        dve.wait_ge(s["mb_full"], b_full(b, f"norm{qt}"))
                        normalise(MB[:, :].rearrange("p (o h w) -> p o h w", o=1, w=VW), rden2[:, :].unsqueeze(1),
                                  O2[:, qt, :].rearrange("p (o h d) -> p o h d", o=1, d=D), 4).then_inc(s["o2_ok"], 1)
                        dve.wait_ge(s["o2_ok"], b * TT + qt + 1)
                        dve.sem_inc(s["mb_free"], 1)
                link(v.tensor_tensor(out=res2[:, :, :], in0=O2[:, :, :], in1=x1[:, :, :], op=ALU.add))
                dve.wait_ge(s["x2all_ok"], b)
                layer_norm(b, res2, st2, mv2, ve2, rs2, x2, TT, s["ve2_ok"], s["rs2_ok"], s["x2_ok"])
                dve.wait_ge(s["mb_full"], b_full(b, "logits"))
                link(v.tensor_tensor(out=logits[:, bass.ds(b * TT, TT), :], in0=MB[:, 0:TT * E].rearrange("p (t e) -> p t e", t=TT),
                                in1=rb_row[:, :].unsqueeze(1).broadcast_to([P, TT, E]), op=ALU.add))
                dve.sem_inc(s["mb_free"], 1)

            before_loop = n[0]
            turn[1] = LINKS_A_BATCH = 19
            with dve.Fori(0, NB) as b:
                turn[0] = b
                body(b)
            assert n[0] - before_loop == LINKS_A_BATCH, n[0] - before_loop
            turn[0] = 0
            n[0] = before_loop + NB * LINKS_A_BATCH

            def bc(ap, axis, shape):
                return ap.unsqueeze(axis).broadcast_to(shape)

            TE = [P, NTK, E]
            link(v.tensor_reduce(out=mx[:, :], in_=logits[:, :, :], axis=AX.X, op=ALU.max))
            link(v.tensor_tensor(out=eq[:, :, :], in0=logits[:, :, :], in1=bc(mx[:, :], 2, TE), op=ALU.is_ge))
            link(v.tensor_tensor(out=cand[:, :, :], in0=eq[:, :, :], in1=bc(iota_e[:, :], 1, TE), op=ALU.mult))
            link(v.tensor_reduce(out=first[:, :], in_=cand[:, :, :], axis=AX.X, op=ALU.min))
            link(v.tensor_tensor(out=oh[:, :, :], in0=bc(iota_e[:, :], 1, TE), in1=bc(first[:, :], 2, TE), op=ALU.is_equal))
            v.tensor_copy(ohb[:, :, :], oh[:, :, :]).then_inc(s["r_a"], 1)
            dve.wait_ge(s["r_full"], 1)
            link(v.tensor_copy(cnt[:, :], MA[:, 64:64 + E]))
            link(v.tensor_tensor(out=gt[:, :, :], in0=bc(cnt[:, :], 2, [P, E, NTK]), in1=bc(iota_c[:, :], 1, [P, E, NTK]), op=ALU.is_gt))
            link(v.tensor_reduce(out=nti[:, :], in_=gt[:, :, :], axis=AX.X, op=ALU.add))
            link(v.tensor_copy(ends[:, :], nti[:, :]))
            for e in range(1, E):
                link(v.tensor_tensor(out=ends[:, e:e + 1], in0=ends[:, e:e + 1], in1=ends[:, e - 1:e], op=ALU.add))
            link(v.tensor_tensor(out=base[:, :], in0=ends[:, :], in1=nti[:, :], op=ALU.subtract))
            link(v.tensor_scalar(base[:, :], base[:, :], float(SLOTS), None, ALU.mult))
            link(v.tensor_tensor(out=pos[:, :, :], in0=MA[:, 0:64].rearrange("p (t e) -> p t e", e=E), in1=bc(base[:, :], 1, TE), op=ALU.add))
            link(v.tensor_tensor(out=pos[:, :, :], in0=pos[:, :, :], in1=oh[:, :, :], op=ALU.mult))
            link(v.tensor_reduce(out=slotf[:, :], in_=pos[:, :, :], axis=AX.X, op=ALU.add))
            v.tensor_copy(slot[:, :], slotf[:, :]).then_inc(s["slot_ok"], 1)
            link(v.tensor_tensor(out=le[:, :, :], in0=bc(ends[:, :], 1, [P, NTILE, E]), in1=bc(iota_t[:, :], 2, [P, NTILE, E]), op=ALU.is_le))
            link(v.tensor_reduce(out=tef[:, :], in_=le[:, :, :], axis=AX.X, op=ALU.add))
            v.tensor_scalar(tile_e[:, :], tef[:, :], float(E - 1), None, ALU.min).then_inc(s["te_ok"], 1)
            with dve.Fori(0, NTILE) as j:
                dve.wait_ge(s["up_full"], j + 1)
                dve.wait_ge(s["bt_in"], 32 * j + 32)
                dve.wait_ge(s["sg_ok"], j)
                v.tensor_tensor(out=gs[:, :], in0=SA[:, 1, :], in1=b1t[:, F:2 * F], op=ALU.add).then_inc(s["gs_ok"], 1)
                dve.wait_ge(s["act_ok"], j)
                v.tensor_tensor(out=aa[:, :], in0=SA[:, 0, :], in1=b1t[:, 0:F], op=ALU.add).then_inc(s["aa_ok"], 1)
                dve.wait_ge(s["aa_ok"], j + 1)
                dve.wait_ge(s["sg_ok"], j + 1)
                dve.wait_ge(s["actT_full"], j)
                v.tensor_tensor(out=act_[:, :], in0=aa[:, :], in1=sg[:, :], op=ALU.mult).then_inc(s["act_ok"], 1)
                dve.wait_ge(s["down_full"], j + 1)
                dve.wait_ge(s["y_out"], 16 * j)
                v.tensor_tensor(out=y[:, :], in0=SB[:, 0, 0:C], in1=b2t[:, :], op=ALU.add).then_inc(s["y_ok"], 1)
            dve.wait_ge(s["gath"], 16 * NTK)
            link(v.tensor_tensor(out=res3[:, :, :], in0=x2all[:, :, :], in1=yg[:, :, :], op=ALU.add))
            layer_norm(0, res3, st3, mv3, ve3, rs3, x3, NTK, s["ve3_ok"], s["rs3_ok"], s["x3_ok"])

        @block.tensor
        def _(pe):
            mm = nc.tensor.matmul

            def tr(dst, src, idn):
                return nc.tensor.transpose(dst, src, idn)

            pe.wait_ge(s["w_in"], 16 * 6)
            pe.wait_ge(s["consts"], 1)
            pe.wait_ge(s["fill"], 1)
            pe.wait_ge(s["er_stacked"], 16 * 14)
            with pe.Fori(0, NB) as b:
                def a_box(use):
                    pe.wait_ge(s["ma_free"], a_full(b, use) - 1)

                def b_box(use):
                    pe.wait_ge(s["mb_free"], b_full(b, use) - 1)

                pe.wait_ge(s["xT_in"], b * 16 + 16)
                for t in range(TT):
                    a_box(f"qkv{t}")
                    mm(MA[:, 0:3 * C], xT[:, t * P:(t + 1) * P], wqkv[:, :], start=True, stop=True).then_inc(s["ma_full"], 1)
                pe.wait_ge(s["cT_in"], b * 16 + 16)
                b_box("kv")
                mm(MB[:, 0:NT], wk[:, :], cT[:, :], start=True, stop=True)
                for t in range(TT):
                    last = mm(MB[:, NT + t * C:NT + (t + 1) * C], cT[:, t * P:(t + 1) * P], wv[:, :], start=True, stop=True)
                last.then_inc(s["mb_full"], 1)
                pe.wait_ge(s["qkn_ok"], b + 1)
                a_box("qkT")
                for w in range(2):
                    for t in range(TT):
                        last = tr(MA[:, w * NT + t * P:w * NT + (t + 1) * P], qkn[:, t, w, :, :].rearrange("p d h -> p (d h)"), ident[:, :])
                last.then_inc(s["ma_full"], 1)
                pe.wait_ge(s["qs_in"], b * 32 + 32)
                pe.wait_ge(s["exp1"], b * 8)
                for u in range(16):
                    hp, qt = divmod(u, 2)
                    pe.wait_ge(s["negm1_ok"], b * 16 + max(u - 1, 0))
                    for i in range(2):
                        h = 2 * hp + i
                        last = mm(SA[:, u % 2, i * NT:(i + 1) * NT], QS[0:96, h, qt * P:(qt + 1) * P], KS[0:96, h, :], start=True, stop=True)
                    last.then_inc(s["sa_full"], 1)
                pe.wait_ge(s["negm1_ok"], b * 16 + 16)
                a_box("shiftT")
                tr(MAb[0:TT * H, 0:P], negm1[:, :, :].rearrange("p q h -> p (q h)"), identb[:, :]).then_inc(s["ma_full"], 1)
                pe.wait_ge(s["m_in"], b * 16 + 16)

                def scores_t(u):
                    pe.wait_ge(s["exp1"], b * 8 + u)
                    for kt in range(TT):
                        for i in range(2):
                            h = 2 * u + i
                            last = mm(SA[:, kt, i * NT:(i + 1) * NT], KS[:, h, kt * P:(kt + 1) * P], QS[:, h, :], start=True, stop=True)
                    last.then_inc(s["st_full"], 1)

                def weigh(grp):
                    pe.wait_ge(s["exp1"], b * 8 + 2 * grp + 2)
                    for kt in range(TT):
                        for i in range(HEADS_A_GROUP):
                            h = grp * HEADS_A_GROUP + i
                            last = mm(MA[VW * i:VW * i + VW, (grp % 2) * NT:(grp % 2 + 1) * NT], V1[:, kt, h, :],
                                      P1[:, grp % 2, kt, i, :], start=(kt == 0), stop=(kt == TT - 1))
                    last.then_inc(s["pv1_done"], 1)

                pe.wait_ge(s["v1_ok"], b + 1)
                for grp in range(NG):
                    for i in range(2):
                        scores_t(2 * grp + i)
                    if grp % 2 == 0:
                        a_box(f"pv{grp // 2}")
                    weigh(grp)
                    if grp % 2:
                        pair = grp // 2
                        pe.wait_ge(s["pv1_done"], b * NG + grp + 1)
                        pe.sem_inc(s["ma_full"], 1)
                        a_box(f"norm{pair}")
                        for qt in range(TT):
                            for g2 in range(2):
                                last = tr(MA[:, qt * 256 + g2 * P:qt * 256 + (g2 + 1) * P],
                                          OT1[:, g2 * NT + qt * P:g2 * NT + (qt + 1) * P], ident[:, :])
                        last.then_inc(s["ma_full"], 1)
                pe.wait_ge(s["o1_ok"], 2 * b + 2)
                a_box("oT")
                for t in range(TT):
                    last = tr(MA[:, t * P:(t + 1) * P], O1[:, t, :], ident[:, :])
                last.then_inc(s["ma_full"], 1)
                a_box("proj")
                for t in range(TT):
                    last = mm(MA[:, t * C:(t + 1) * C], O1T[:, t * P:(t + 1) * P], wproj[:, :], start=True, stop=True)
                last.then_inc(s["ma_full"], 1)
                pe.wait_ge(s["x1_ok"], b + 1)
                a_box("x1T")
                for t in range(TT):
                    last = tr(MA[:, t * P:(t + 1) * P], x1[:, t, :], ident[:, :])
                last.then_inc(s["ma_full"], 1)
                a_box("q2T")
                mm(MA[:, 0:NT], wq[:, :], x1T[:, :], start=True, stop=True).then_inc(s["ma_full"], 1)

                def scores(qb):
                    if qb >= 2:
                        pe.wait_ge(s["exp2"], b * NQB + qb - 1)
                    for kt in range(1 if qb < 4 else 2):
                        bank = SB[:, 2 * (qb % 2) + kt, :].rearrange("p (h q) -> p h q", h=H)
                        for h in range(H):
                            mm(bank[:, h, :], KS2[:, h, kt * P:(kt + 1) * P], Z[:, h, QB * qb:QB * (qb + 1)],
                               start=(h == 0), stop=False, skip_group_check=True)
                        for q in range(0, QB, 2):
                            w = NT - 1 - (QB * qb + q) + kt * P
                            last = mm(bank[:, :, q:q + 2], ErS[:, w:w + P], Z[:, :, QB * qb + q:QB * qb + q + 2],
                                      start=False, stop=False, skip_group_check=True)
                    last.then_inc(s["sc_full"], 1)

                def shift(qb):
                    if qb < 4:
                        pe.wait_ge(s["copied"], b * NQB + qb + 1)
                        src = Sb
                    else:
                        pe.wait_ge(s["maxed"], b * 4 + qb - 3)
                        src = Sm
                    b_box(f"tr{qb}")
                    for c in range(4):
                        last = tr(MBb[:, c * P:(c + 1) * P], src[:, qb % 2, c * P:(c + 1) * P], identb[:, :])
                    last.then_inc(s["mb_full"], 1)
                    pe.wait_ge(s["negm2_ok"], b * NQB + qb + 1)
                    for kt in range(1 if qb < 4 else 2):
                        for c in range(4):
                            last = mm(SB[:, 2 * (qb % 2) + kt, c * P:(c + 1) * P], negm2[:, qb, c:c + 1].broadcast_to([P, P]),
                                      identb[:, :], start=False, stop=True, skip_group_check=True)
                    last.then_inc(s["shifted"], 1)

                pe.wait_ge(s["z_ok"], b + 1)
                scores(0)
                for qb in range(NQB):
                    if qb + 1 < NQB:
                        scores(qb + 1)
                    shift(qb)
                    if qb % 4 == 3:
                        qt = qb // 4
                        pe.wait_ge(s["exp2"], b * NQB + qb + 1)
                        pe.wait_ge(s["v2_ok"], b + 1)
                        b_box(f"pv{qt}")
                        for grp in range(NG):
                            for kt in range(qt + 1):
                                for i in range(HEADS_A_GROUP):
                                    h = grp * HEADS_A_GROUP + i
                                    rhs = P2a[:, h, :] if qt == 0 else P2b[:, kt, h, :]
                                    last = mm(MB[VW * i:VW * i + VW, grp * P:(grp + 1) * P], V2[:, kt, h, :], rhs,
                                              start=(kt == 0), stop=(kt == qt))
                        last.then_inc(s["pv2_done"], 1)
                        pe.wait_ge(s["pv2_done"], b * TT + qt + 1)
                        pe.sem_inc(s["mb_full"], 1)
                        b_box(f"norm{qt}")
                        for grp in range(NG):
                            last = tr(MB[:, grp * P:(grp + 1) * P], OT2[:, grp * P:(grp + 1) * P], ident[:, :])
                        last.then_inc(s["mb_full"], 1)
                pe.wait_ge(s["x2_ok"], b + 1)
                b_box("x2T")
                for t in range(TT):
                    last = tr(MB[:, t * P:(t + 1) * P], x2[:, t, :], ident[:, :])
                last.then_inc(s["mb_full"], 1)
                b_box("logits")
                for t in range(TT):
                    last = mm(MB[:, t * E:(t + 1) * E], x2T[:, t * P:(t + 1) * P], wr[:, :], start=True, stop=True)
                last.then_inc(s["mb_full"], 1)
            pe.wait_ge(s["r_a"], 1)
            mm(MA[:, 0:NTK * E], before[:, :], ohb[:, :, :].rearrange("p t e -> p (t e)"), start=True, stop=False, skip_group_check=True)
            for t in range(NTK):
                for u in range(t + 1, NTK):
                    mm(MA[:, u * E:(u + 1) * E], ones_b[:, :], ohb[:, t, :], start=False, stop=False, skip_group_check=True)
                last = mm(MA[:, NTK * E:NTK * E + E], ones_b[:, :], ohb[:, t, :], start=False, stop=(t == NTK - 1), skip_group_check=True)
            last.then_inc(s["r_full"], 1)
            pe.wait_ge(s["te_ok"], 1)
            pe.wait_ge(s["bigw"], 32)
            with pe.Fori(0, NTILE) as j:
                e = pe.value_load(tile_e[0:1, bass.ds(j, 1)], min_val=0, max_val=E - 1)
                pe.wait_ge(s["xg_in"], 16 * j + 16)
                pe.wait_ge(s["xgT_ok"], j)
                tr(MA[:, 0:P], xg[:, :], ident[:, :]).then_inc(s["xgT_full"], 1)
                pe.wait_ge(s["xgT_ok"], j + 1)
                pe.wait_ge(s["aa_ok"], j)
                for k in (1, 0):
                    last = mm(SA[:, k, :], xgT[:, :], w1_sb[:, bass.ds(e, 1), k * F:(k + 1) * F].rearrange("p o f -> p (o f)"), start=True, stop=True)
                last.then_inc(s["up_full"], 1)
                pe.wait_ge(s["act_ok"], j + 1)
                pe.wait_ge(s["actT_ok"], j)
                for k in range(F // P):
                    last = tr(MB[:, k * P:(k + 1) * P], act_[:, k * P:(k + 1) * P], ident[:, :])
                last.then_inc(s["actT_full"], 1)
                pe.wait_ge(s["actT_ok"], j + 1)
                pe.wait_ge(s["y_ok"], j)
                for k in range(F // P):
                    last = mm(SB[:, 0, 0:C], actT[:, k * P:(k + 1) * P], w2_sb[:, bass.ds(e, 1), k, :].rearrange("p o c -> p (o c)"), start=(k == 0), stop=(k == F // P - 1))
                last.then_inc(s["down_full"], 1)


def kernel(**inputs):
    import numpy as np
    import concourse.bacc as bacc
    from concourse.bass_utils import run_bass_kernel_spmd as run

    def cols(a):
        return np.asarray(a).transpose(0, 2, 1)

    def by_part(w):
        w = np.asarray(w)
        return w.reshape((H, D) + w.shape[1:]).swapaxes(0, 1).reshape(w.shape)

    i = {k: np.asarray(v) for k, v in inputs.items()}
    arrays = {
        "x_rows": i["x"].reshape(NB, TT, P, C).transpose(0, 2, 1, 3),
        "x_cols": cols(i["x"]),
        "ctx_cols": cols(i["ctx_1024"]),
        "wqkv_t": i["L0_attn_qkv_w"].T,
        "temperature": i["L0_attn_temperature"].reshape(H),
        "wproj_t": i["L0_attn_proj_w"].T,
        "proj_b": i["L0_attn_proj_b"],
        "wq_t": by_part(i["L0_xattn_Wq"]).T,
        "bq": by_part(i["L0_xattn_bq"]),
        "wk_t": by_part(i["L0_xattn_Wk"]).T,
        "bk": by_part(i["L0_xattn_bk"]),
        "wv_t": i["L0_xattn_Wv"].T,
        "bv": i["L0_xattn_bv"],
        "er_t": i["L0_xattn_Er"].T,
        "router_w": i["L0_ffn_router_w"],
        "router_b": i["L0_ffn_router_b"],
        "w1": i["L0_ffn_w1"],
        "b1": i["L0_ffn_b1"],
        "w2": i["L0_ffn_w2"],
        "b2": i["L0_ffn_b2"],
    }
    arrays = {k: np.ascontiguousarray(v) for k, v in arrays.items()}
    nc = bacc.Bacc("TRN2", target_bir_lowering=False, num_devices=1)
    args = [nc.dram_tensor("in_" + k, a.shape, FP32, kind="ExternalInput").ap() for k, a in arrays.items()]
    out = nc.dram_tensor("out", (NB, NT, C), FP32, kind="ExternalOutput").ap()
    build(nc, *args, out)
    r = run(nc, [{"in_" + k: a for k, a in arrays.items()}], core_ids=[0])
    return r.results[0]["out"]
```

```python
from contextlib import ExitStack

import concourse.bass as bass
from concourse import mybir

FP32 = mybir.dt.float32
BF16 = mybir.dt.bfloat16
I32 = mybir.dt.int32
U32 = mybir.dt.uint32
ALU = mybir.AluOpType
ACT = mybir.ActivationFunctionType
AX = mybir.AxisListType

LINKS_A_TURN = 20
NB, NT, C = 4, 256, 128
H, D = 16, 8
P = 128
TT = NT // P
NTK = NB * TT
HEADS_A_GROUP = 4
NG = H // HEADS_A_GROUP
VW = 32
NTERM = 6
SR = NTERM * D
QB = 32
NQB = NT // QB
E, F = 8, 512
SLOTS = P
NTILE = NB * TT + E - 1
LN_EPS = 1e-5
MASKED = -1e30

STEPS = tuple(x.split(".") for x in """
    B.v A1.qkv B.build A1.qkn B.sc0 A1.qkT
    B.tr0 B.sc1 B.sh0 A2.st0 A2.xpb
    B.tr1 B.sc2 B.sh1 A2.st1 A2.pv0 A2.st2
    B.tr2 B.sc3 B.sh2 A2.st3 A2.pv1 A2.k2T
    B.tr3 B.sc4 B.sh3 A2.st4 A2.nm0 B.pv0 A2.st5
    B.tr4 B.nm0 B.sc5 B.sh4 A2.pv2 A2.st6 A2.st7
    B.tr5 B.sc6 B.sh5 A2.pv3 A2.nm1 A1.qsin A2.oT A1.vcp
    B.tr6 B.sc7 B.sh6 A1.d0 A1.d1 A2.proj A1.d2 A1.d3 A2.ln1
    B.tr7 B.sh7 A1.d4 A1.d5 A2.x1T A1.d6 A1.d7 A2.q2T A1.d8 A1.d9
    B.pv1 A1.d10 A1.d11 B.nm1 A1.d12 A1.d13 B.ln2 A1.d14 A1.d15 B.x2T A1.shT B.lg
""".split())
TURNS = NB + 2
FIRST_FULL, PAST_FULL = 2, NB

A_FILLS = {"A1.qkv": ("qkv0", "qkv1"), "A1.qkT": ("qkT",), "A2.pv1": ("pv0",), "A2.nm0": ("norm0",), "A2.k2T": ("k2T",),
           "A2.pv3": ("pv1",), "A2.nm1": ("norm1",), "A2.oT": ("oT",), "A2.proj": ("proj",), "A2.x1T": ("x1T",),
           "A2.q2T": ("q2T",), "A1.shT": ("shiftT",)}
B_FILLS = {"B.v": ("v",), **{f"B.tr{q}": (f"tr{q}",) for q in range(NQB)}, "B.pv0": ("pv0",), "B.pv1": ("pv1",),
           "B.nm0": ("norm0",), "B.nm1": ("norm1",), "B.x2T": ("x2T",), "B.lg": ("logits",)}


def stages(t):
    return [n for n, b in (("A1", t), ("A2", t - 1), ("B", t - 2)) if 0 <= b < NB]


def fills(table, held):
    return [f for stage, step in STEPS if stage in held for f in table.get(f"{stage}.{step}", ())]


A_FULL_TURN = len(fills(A_FILLS, ("A1", "A2")))
B_BOX = fills(B_FILLS, ("B",))


def a_full(t, use):
    if isinstance(t, int) and not (1 <= t < NB):
        before = 0 if t == 0 else len(fills(A_FILLS, ("A1",))) + (NB - 1) * A_FULL_TURN
        return before + fills(A_FILLS, stages(t)).index(use) + 1
    return len(fills(A_FILLS, ("A1",))) + (t - 1) * A_FULL_TURN + fills(A_FILLS, ("A1", "A2")).index(use) + 1


def b_full(b, use):
    return b * len(B_BOX) + B_BOX.index(use) + 1


def build(nc, x_rows, x_cols, ctx_cols, wqkv_t, temperature, wproj_t, proj_b, wq_t, bq, wk_t, bk, wv_t, bv,
          er_t, router_w, router_b, w1, b1, w2, b2, out):
    ctx = ExitStack()
    with ctx:
        def sb(name, shape, dt=FP32):
            return ctx.enter_context(nc.sbuf_tensor(name, shape, dt))

        def pb(name, shape, dt=FP32):
            return ctx.enter_context(nc.psum_tensor(name, shape, dt))

        def sem(name):
            return ctx.enter_context(nc.semaphore(name))

        def dram(name, shape, dt=FP32):
            return nc.dram_tensor(name, shape, dt, kind="Internal").ap()

        parts_a = dram("parts_a", (2, NTERM, P, NT), BF16)
        parts_b = dram("parts_b", (2, NTERM, P, NT), BF16)
        shift_a = dram("shift_a", (NB, TT, H, P), BF16)
        sorted_x = dram("sorted_x", (NTILE * SLOTS, C))
        sorted_y = dram("sorted_y", (NTILE * SLOTS, C))

        ident = sb("ident", [P, P])
        identb = sb("identb", [P, P], BF16)
        ones_b = sb("ones_b", [P, P], BF16)
        before = sb("before", [P, P], BF16)
        parity = sb("parity", [P, NT], BF16)
        pad = sb("pad", [P, 1])
        half = sb("half", [P, NTK])
        wqkv = sb("wqkv", [P, 3 * C])
        wproj = sb("wproj", [P, C])
        wq = sb("wq", [P, C])
        wk = sb("wk", [P, C])
        wv = sb("wv", [P, C])
        wr = sb("wr", [P, E])
        pbias = sb("pbias", [P, C])
        bv_row = sb("bv_row", [P, C])
        rb_row = sb("rb_row", [P, E])
        bq_col = sb("bq_col", [P, 1])
        bk_col = sb("bk_col", [P, 1])
        temp = sb("temp", [P, H])
        trow = sb("trow", [P, D, H])
        er_parts = sb("er_parts", [D, 3, NT], BF16)
        er_mask = sb("er_mask", [1, 2 * NT], BF16)
        EW = 400
        ErS = sb("ErS", [P, EW], BF16)
        w1_sb = sb("w1_sb", [P, E, 2 * F])
        w2_sb = sb("w2_sb", [P, E, F // P, C])

        xT = sb("xT", [P, NT])
        x_tok = sb("x_tok", [P, TT, C])
        xpb = sb("xpb", [P, TT, C])
        qkv = sb("qkv", [P, TT, 3 * C])
        sq = sb("sq", [P, 4, C], BF16)
        n2 = sb("n2", [P, 4])
        n2c = sb("n2c", [P, 4])
        rn = sb("rn", [P, 4])
        qkn = sb("qkn", [P, TT, 2, D, H])
        qkT = sb("qkT", [P, 2, NT])
        restA = sb("restA", [P, 2, NT])
        SpA = sb("SpA", [P, 3, 2, NT], BF16)
        V1 = sb("V1", [P, TT, H, VW])
        QS = sb("QS", [P, H, NT], BF16)
        KS = sb("KS", [P, H, NT], BF16)
        negm1 = sb("negm1", [P, TT, H], BF16)
        nmT = sb("nmT", [TT * H, P], BF16)
        P1 = sb("P1", [P, 2, TT, HEADS_A_GROUP, NT])
        OT1 = sb("OT1", [P, 2 * NT])
        rden1 = sb("rden1", [P, TT, 2 * HEADS_A_GROUP])
        O1 = sb("O1", [P, TT, C])
        O1T = sb("O1T", [P, NT])
        res1 = sb("res1", [P, TT, C])
        st1 = sb("st1", [P, TT, 6])
        mv1 = sb("mv1", [P, TT, 2])
        ve1 = sb("ve1", [P, TT])
        rs1 = sb("rs1", [P, TT])
        x1 = sb("x1", [P, TT, C])
        x1T = sb("x1T", [P, NT])
        x1k = sb("x1k", [P, TT, C])

        cT = sb("cT", [P, NT])
        qk2T = sb("qk2T", [P, 2, NT])
        restB = sb("restB", [P, 2, NT])
        SpB = sb("SpB", [P, 3, 2, NT], BF16)
        V2 = sb("V2", [P, TT, H, VW])
        QZ = sb("QZ", [P, H, NT], BF16)
        KZ = sb("KZ", [P, H, NT], BF16)
        Z = sb("Z", [P, H, NT], BF16)
        KS2 = sb("KS2", [P, H, NT], BF16)
        Sb = sb("Sb", [P, 2, 512], BF16)
        Sm = sb("Sm", [P, 2, 512], BF16)
        negm2 = sb("negm2", [P, NQB, 4], BF16)
        P2a = sb("P2a", [P, H, P])
        P2b = sb("P2b", [P, 2, H, P])
        er = P2a[0:D, 0:2, :].rearrange("d h q -> d (h q)")
        er_rest = P2a[0:D, 2:4, :].rearrange("d h q -> d (h q)")
        OT2 = sb("OT2", [P, 512])
        rden2 = sb("rden2", [P, H])
        O2 = sb("O2", [P, TT, C])
        res2 = sb("res2", [P, TT, C])
        st2 = sb("st2", [P, TT, 6])
        mv2 = sb("mv2", [P, TT, 2])
        ve2 = sb("ve2", [P, TT])
        rs2 = sb("rs2", [P, TT])
        x2 = sb("x2", [P, TT, C])
        x2T = sb("x2T", [P, NT])
        x2all = sb("x2all", [P, NB * TT, C])
        logits = sb("logits", [P, NB * TT, E])

        iota_e = sb("iota_e", [P, E])
        iota_t = sb("iota_t", [P, NTILE])
        iota_c = sb("iota_c", [P, NTK])
        mx = sb("mx", [P, NTK])
        eq = sb("eq", [P, NTK, E])
        cand = sb("cand", [P, NTK, E])
        first = sb("first", [P, NTK])
        oh = sb("oh", [P, NTK, E])
        ohb = sb("ohb", [P, NTK, E], BF16)
        cnt = sb("cnt", [P, E])
        gt = sb("gt", [P, E, NTK])
        nti = sb("nti", [P, E])
        ends = sb("ends", [P, E])
        base = sb("base", [P, E])
        pos = sb("pos", [P, NTK, E])
        slotf = sb("slotf", [P, NTK])
        slot = sb("slot", [P, NTK], I32)
        le = sb("le", [P, NTILE, E])
        tef = sb("tef", [P, NTILE])
        tile_e = sb("tile_e", [P, NTILE], I32)

        QZr = QZ[:, :, :].rearrange("p h t -> p (h t)").bitcast(FP32)
        KZr = KZ[:, :, :].rearrange("p h t -> p (h t)").bitcast(FP32)
        zrow = sb("zrow", [P, C])
        def rooms(tile, spec):
            at, got = 0, []
            for n_, width in spec:
                got.append(tile[:, at:at + n_ * width].rearrange("p (n w) -> p n w", w=width))
                at += n_ * width
            return got

        b1t, xg = rooms(P2b[:, :, :, :].rearrange("p k h q -> p (k h q)"), ((2, 2 * F), (2, C)))
        aa, gs, act_, xgT, b2t, y = rooms(P1[:, :, :, :, :].rearrange("p g k h q -> p (g k h q)"),
                                          ((2, F), (2, F), (2, F), (2, P), (2, C), (2, C)))
        sg, actT = rooms(P2a[:, :, :].rearrange("p h q -> p (h q)"), ((2, F), (2, F)))
        yg, res3 = rooms(QZr, ((NTK, C), (NTK, C)))
        x3, = rooms(KZr, ((NTK, C),))
        st3 = sb("st3", [P, NTK, 6])
        mv3 = sb("mv3", [P, NTK, 2])
        ve3 = sb("ve3", [P, NTK])
        rs3 = sb("rs3", [P, NTK])

        SA = pb("SA", [P, 2, 512])
        MA = pb("MA", [P, 512])
        SB = pb("SB", [P, 4, 512])
        MB = pb("MB", [P, 512])
        MAb = MA[:, :].bitcast(BF16)
        MBb = MB[:, :].bitcast(BF16)
        UP = ([SA[:, 0, :], SA[:, 1, :]], [SB[:, 0, :], SB[:, 1, :]])

        s = {n: sem(n) for n in (
            "wqkv_in", "w_in", "temp_in", "c_in", "er_in", "fill", "ident_ok", "consts", "er_split", "er_stacked", "zero_out", "bigw",
            "dchain", "pchain",
            "ma_full", "ma_free", "mb_full", "mb_free",
            "xT_in", "xtok_in", "n2_ok", "n2c_ok", "rn_ok", "qkn_ok", "v1_ok", "xpb_ok", "spa_ok", "pa_out", "qs_in",
            "sa_full", "negm1_ok", "m_out", "m_in", "st_full", "exp1", "ve1_ok", "rs1_ok", "x1_ok",
            "cT_in", "spk_ok", "spq_ok", "pk_out", "pq_out", "kz_in", "qz_in", "z_ok", "sc_full", "copied", "maxed", "shifted",
            "exp2", "ve2_ok", "rs2_ok", "x2_ok", "x2all_ok",
            "oh_ok", "ranked", "slot_ok", "te_ok", "scat", "xg_in0", "xg_in1", "bt_in0", "bt_in1", "xgT_full", "xgT_ok", "up_full", "gs_ok", "aa_ok",
            "sg_ok", "act_ok", "actT_full", "actT_ok", "down_full", "y_ok", "y_out0", "y_out1", "gath", "ve3_ok", "rs3_ok", "x3_ok", "o_out",
        )}
        block = ctx.enter_context(nc.Block())

        def wait(eng, name, value):
            if not (isinstance(value, int) and value <= 0):
                eng.wait_ge(s[name], value)

        def turns(eng, steps, looped=None):
            def turn(t, held):
                batch = {"A1": t, "A2": t - 1, "B": t - 2}
                for stage, step in STEPS:
                    name, index = step.rstrip("0123456789"), step[len(step.rstrip("0123456789")):]
                    if stage in held and (stage, name) in steps:
                        steps[stage, name](t, batch[stage], *([int(index)] if index else []))
            for t in range(FIRST_FULL):
                turn(t, stages(t))
            with eng.Fori(FIRST_FULL, PAST_FULL) as t:
                if looped:
                    looped(t)
                turn(t, stages(FIRST_FULL))
            if looped:
                looped(None)
            for t in range(PAST_FULL, TURNS):
                turn(t, stages(t))

        def tile_turns(eng, rows, middle, end):
            def turn(j, par, before=True, after=True):
                middle(j, par)
                if after and rows:
                    rows(j + 1, 1 - par)
                if before:
                    end(j - 1, 1 - par)

            if rows:
                rows(0, 0)
            turn(0, 0, before=False)
            turn(1, 1)
            turn(2, 0)
            with eng.Fori(3, NTILE - 2, 2) as j:
                turn(j, 1)
                turn(j + 1, 0)
            turn(NTILE - 2, 1)
            turn(NTILE - 1, 0, after=False)
            end(NTILE - 1, 0)

        def of_parity(j, par, each):
            return (j - par) * (each // 2) + each

        def one(ap):
            return ap.squeeze(0)

        @block.sync
        def _(sp):
            def load(dst, src, name):
                sp.dma_start(dst, src).then_inc(s[name], 16)

            load(xT[:, :], x_cols[0], "xT_in")
            load(wqkv[:, :], wqkv_t, "wqkv_in")
            load(temp[:, :], temperature.partition_broadcast(P), "temp_in")
            load(er[:, :], er_t, "er_in")
            load(pbias[:, :], proj_b.partition_broadcast(P), "c_in")
            load(bv_row[:, :], bv.partition_broadcast(P), "c_in")
            load(rb_row[:, :], router_b.partition_broadcast(P), "c_in")
            load(bq_col[:, :], bq.unsqueeze(1), "c_in")
            load(bk_col[:, :], bk.unsqueeze(1), "c_in")
            load(wproj[:, :], wproj_t, "w_in")
            load(wq[:, :], wq_t, "w_in")
            load(wk[:, :], wk_t, "w_in")
            load(wv[:, :], wv_t, "w_in")
            load(wr[:, :], router_w, "w_in")

            def write_parts(dst, Sp, which, rows, name):
                for at, n, first in rows:
                    src = Sp[:, first, which, :].unsqueeze(1).broadcast_to([P, n, NT]) if which else Sp[:, first:first + n, 0, :]
                    load(dst[which, at:at + n].rearrange("w p t -> p w t"), src, name)

            Q_ROWS = ((0, 3, 0), (3, 2, 0), (5, 1, 0))
            K_ROWS = ((0, 3, 0), (3, 2, 1), (5, 1, 2))

            def stack(parts, which):
                return parts[which].rearrange("w (d h) t -> (w d) h t", h=H)

            def of_batch(t_, b):
                return one(t_[bass.ds(b, 1)] if not isinstance(b, int) else t_[b:b + 1])

            def next_x(t, b):
                wait(sp, "ma_full", a_full(t, "qkv1"))
                load(xT[:, :], of_batch(x_cols, (t + 1) % NB), "xT_in")

            def q_k_out(t, b):
                wait(sp, "qs_in", b * 32)
                wait(sp, "spa_ok", b + 1)
                for which, rows in ((0, Q_ROWS), (1, K_ROWS)):
                    write_parts(parts_a, SpA, which, rows, "pa_out")

            def q_k_in(t, b):
                wait(sp, "st_full", b * 8)
                wait(sp, "pa_out", b * 96 + 96)
                for which, st in ((0, QS), (1, KS)):
                    load(st[0:SR, :, :], stack(parts_a, which), "qs_in")

            def shift_rows(t, b):
                wait(sp, "ma_free", a_full(t, "shiftT"))
                sh = of_batch(shift_a, b)
                load(sh.rearrange("q h t -> (q h) t"), nmT[:, :], "m_out")
                wait(sp, "m_out", b * 16 + 16)
                load(QS[96:97, :, :].rearrange("o h (q t) -> o h q t", q=TT), sh.rearrange("q h t -> h q t").unsqueeze(0), "m_in")

            def context(t, b):
                if not isinstance(b, int) or b > 0:
                    wait(sp, "mb_full", b_full(b - 1, "v"))
                load(cT[:, :], of_batch(ctx_cols, b), "cT_in")

            def residual_in(t, b):
                wait(sp, "xpb_ok", b)
                load(x_tok[:, :, :], of_batch(x_rows, b), "xtok_in")

            def cross_parts(t, b, which, rows, Zin, ready, done_out, done_in):
                wait(sp, done_in, b * 32)
                wait(sp, ready, b + 1)
                write_parts(parts_b, SpB, which, rows, done_out)
                wait(sp, done_out, b * 48 + 48)
                wait(sp, "z_ok", b)
                for half_ in (0, 64):
                    load(Zin[half_:half_ + SR, :, :], stack(parts_b, which), done_in)

            turns(sp, {
                ("A1", "qkv"): next_x, ("A1", "qkT"): q_k_out, ("A1", "qsin"): q_k_in, ("A1", "shT"): shift_rows,
                ("A2", "st"): lambda t, b, u: context(t, b) if u == 0 else None,
                ("A2", "xpb"): residual_in,
                ("A2", "k2T"): lambda t, b: cross_parts(t, b, 1, K_ROWS, KZ, "spk_ok", "pk_out", "kz_in"),
                ("A2", "q2T"): lambda t, b: cross_parts(t, b, 0, Q_ROWS, QZ, "spq_ok", "pq_out", "qz_in"),
            })
            sp.wait_ge(s["te_ok"], 1)
            sp.wait_ge(s["scat"], 16 * NTK)

            def tile_in(j, par, out_too=True):
                e = sp.value_load(tile_e[0:1, bass.ds(j, 1)], min_val=0, max_val=E - 1)
                wait(sp, "xgT_full", j - 1)
                load(xg[:, par, :], sorted_x[bass.ds(j * SLOTS, SLOTS), :], f"xg_in{par}")
                if out_too:
                    tile_out(j - 2, par)
                load(b1t[:, par, :], one(b1[bass.ds(e, 1), :]).partition_broadcast(P), f"bt_in{par}")
                load(b2t[:, par, :], one(b2[bass.ds(e, 1), :]).partition_broadcast(P), f"bt_in{par}")

            def tile_out(j, par):
                wait(sp, "y_ok", j + 1)
                load(sorted_y[bass.ds(j * SLOTS, SLOTS), :], y[:, par, :], f"y_out{par}")

            tile_in(0, 0, out_too=False)
            tile_in(1, 1, out_too=False)
            tile_in(2, 0)
            with sp.Fori(3, NTILE - 1, 2) as j:
                tile_in(j, 1)
                tile_in(j + 1, 0)
            tile_out(NTILE - 2, 1)
            tile_out(NTILE - 1, 0)
            sp.wait_ge(s["x3_ok"], 1)
            load(out.rearrange("b (t p) c -> p (b t) c", p=P), x3[:, :, :], "o_out")
            sp.wait_ge(s["o_out"], 16)

        @block.gpsimd
        def _(pool):
            n = [0]

            def link(ins):
                ins.then_inc(s["pchain"], 1)
                n[0] += 1
                pool.wait_ge(s["pchain"], n[0])

            g = nc.gpsimd
            link(g.memset(half[:, :], -0.5))
            link(g.memset(zrow[:, :], 0.0))
            link(g.memset(ident[:, :], 0.0))
            g.affine_select(out=ident[:, :], in_=ident[:, :], compare_op=ALU.not_equal, fill=1.0,
                            base=0, pattern=[[-1, P]], channel_multiplier=1).then_inc(s["ident_ok"], 1)
            pool.wait_ge(s["ident_ok"], 1)
            g.tensor_copy(identb[:, :], ident[:, :]).then_inc(s["consts"], 1)
            pool.dma_start(w1_sb[:, :, :], w1.rearrange("e c f -> c e f")).then_inc(s["bigw"], 16)
            pool.dma_start(w2_sb[:, :, :, :], w2.rearrange("e (k f) c -> f e k c", f=P)).then_inc(s["bigw"], 16)
            pool.wait_ge(s["er_split"], 1)
            for half_, at in ((0, 0), (64, 1)):
                for blk, w in enumerate((0, 0, 0, 1, 1, 2)):
                    pool.dma_start(ErS[half_ + D * blk:half_ + D * blk + D, at:at + NT], er_parts[:, w, :]).then_inc(s["er_stacked"], 16)
                pool.dma_start(ErS[half_ + SR:half_ + SR + 1, NT + at:NT + at + 140], er_mask[:, NT:NT + 140]).then_inc(s["er_stacked"], 16)
            link(g.memset(before[:, :], 1.0))
            link(g.affine_select(out=before[:, :], in_=before[:, :], compare_op=ALU.is_gt, fill=0.0,
                                 base=0, pattern=[[1, P]], channel_multiplier=-1))
            link(g.iota(iota_e[:, :], pattern=[[1, E]], base=-E, channel_multiplier=0, allow_small_or_imprecise_dtypes=True))
            link(g.iota(iota_t[:, :], pattern=[[1, NTILE]], base=0, channel_multiplier=0, allow_small_or_imprecise_dtypes=True))
            g.iota(iota_c[:, :], pattern=[[SLOTS, NTK]], base=0, channel_multiplier=0, allow_small_or_imprecise_dtypes=True).then_inc(s["consts"], 1)
            pool.dma_start(sorted_x.rearrange("(j p) c -> p j c", p=P),
                           zrow[:, :].unsqueeze(1).broadcast_to([P, NTILE, C])).then_inc(s["zero_out"], 16)

            def root(dst, src, needs, ready, count):
                wait(pool, needs, count)
                g.tensor_tensor(out=dst, in0=src, in1=half[:, 0:src.shape[1]], op=ALU.pow).then_inc(s[ready], 1)

            def add_bias(t, b):
                wait(pool, "xtok_in", b * 16 + 16)
                pool.wait_ge(s["c_in"], 16 * 5)
                if not isinstance(b, int) or b > 0:
                    wait(pool, "ma_free", a_full(t - 1, "proj"))
                g.tensor_tensor(out=xpb[:, :, :], in0=x_tok[:, :, :],
                                in1=pbias[:, :].unsqueeze(1).broadcast_to([P, TT, C]), op=ALU.add).then_inc(s["xpb_ok"], 1)

            turns(pool, {
                ("A1", "qkn"): lambda t, b: root(rn[:, :], n2c[:, :], "n2c_ok", "rn_ok", b + 1),
                ("A2", "xpb"): add_bias,
                ("A2", "ln"): lambda t, b, _: root(rs1[:, :], ve1[:, :], "ve1_ok", "rs1_ok", b + 1),
                ("B", "ln"): lambda t, b, _: root(rs2[:, :], ve2[:, :], "ve2_ok", "rs2_ok", b + 1),
            })
            pool.wait_ge(s["slot_ok"], 1)
            pool.wait_ge(s["zero_out"], 16)
            pool.wait_ge(s["x2all_ok"], NB)
            for t in range(NTK):
                pool.indirect_dma_start(out=sorted_x, out_offset=bass.IndirectOffsetOnAxis(ap=slot[:, t:t + 1], axis=0),
                                        in_=x2all[:, t, :], in_offset=None).then_inc(s["scat"], 16)
            for par in range(2):
                pool.wait_ge(s[f"y_out{par}"], 16 * ((NTILE + 1 - par) // 2))
            for t in range(NTK):
                pool.indirect_dma_start(out=yg[:, t, :], out_offset=None, in_=sorted_y,
                                        in_offset=bass.IndirectOffsetOnAxis(ap=slot[:, t:t + 1], axis=0)).then_inc(s["gath"], 16)
            root(rs3[:, :], ve3[:, :], "ve3_ok", "rs3_ok", 1)

        @block.scalar
        def _(act):
            a = nc.scalar

            def copy(dst, src):
                return a.activation(dst, src, ACT.Copy)

            def a_out(t, use, dst, src):
                wait(act, "ma_full", a_full(t, use))
                copy(dst, src).then_inc(s["ma_free"], 1)

            def b_out(b, use, dst, src):
                wait(act, "mb_full", b_full(b, use))
                copy(dst, src).then_inc(s["mb_free"], 1)

            def qkv_out(t, b):
                wait(act, "qkn_ok", b)
                for i in range(TT):
                    a_out(t, f"qkv{i}", qkv[:, i, :], MA[:, 0:3 * C])
                wait(act, "ma_free", a_full(t, "qkv1"))
                for i in range(TT):
                    for k in range(2):
                        ins = a.activation(sq[:, 2 * i + k, :], qkv[:, i, k * C:(k + 1) * C], ACT.Square,
                                           accum_out=n2[:, 2 * i + k:2 * i + k + 1])
                ins.then_inc(s["n2_ok"], 1)

            def qkT_out(t, b):
                wait(act, "spa_ok", b)
                a_out(t, "qkT", qkT[:, :, :], MA[:, :].rearrange("p (w t) -> p w t", w=2))

            def values(t, b):
                a.activation(V1[:, :, :, 0:D], qkv[:, :, 2 * C:3 * C].rearrange("p t (h d) -> p t h d", d=D), ACT.Copy)\
                    .then_inc(s["v1_ok"], 1)

            def shifts(t, b):
                wait(act, "m_out", b * 16)
                a_out(t, "shiftT", nmT[:, :], MAb[0:TT * H, 0:P])

            def exp1(t, b, u):
                grp, i = divmod(u, 2)
                wait(act, "st_full", b * 8 + u + 1)
                if u == 4:
                    wait(act, "ma_full", a_full(t, "pv0"))
                a.activation(P1[:, grp % 2, :, 2 * i:2 * i + 2, :].rearrange("p k h t -> p k (h t)"),
                             SA[:, :, :], ACT.Exp).then_inc(s["exp1"], 1)

            def weighed1(t, b, grp):
                if grp % 2:
                    a_out(t, f"pv{grp // 2}", OT1[:, :], MA[:, :])

            def copy_scores(t, b, qb):
                wait(act, "sc_full", b * NQB + qb + 1)
                if qb >= 2:
                    wait(act, "mb_full", b_full(b, f"tr{qb - 2}"))
                if qb >= 6:
                    wait(act, "maxed", b * 4 + qb - 5)
                copy(Sb[:, qb % 2, :], SB[:, 2 * (qb % 2), :]).then_inc(s["copied"], 1)

            def exp2(t, b, qb):
                wait(act, "shifted", b * NQB + qb + 1)
                qs, at = slice(QB * (qb % 4), QB * (qb % 4) + QB), 2 * (qb % 2)
                if qb < 4:
                    a.activation(P2a[:, :, qs], SB[:, at, :].rearrange("p (h q) -> p h q", h=H), ACT.Exp)\
                        .then_inc(s["exp2"], 1)
                else:
                    a.activation(P2b[:, :, :, qs].rearrange("p k h q -> p (k h) q"),
                                 SB[:, at:at + 2, :].rearrange("p k (h q) -> p (k h) q", h=H), ACT.Exp).then_inc(s["exp2"], 1)

            def keep_x2(t, b, _):
                wait(act, "x2_ok", b + 1)
                dst = x2all[:, bass.ds(b * TT, TT), :] if not isinstance(b, int) else x2all[:, b * TT:(b + 1) * TT, :]
                copy(dst, x2[:, :, :]).then_inc(s["x2all_ok"], 1)

            turns(act, {
                ("A1", "qkv"): qkv_out, ("A1", "qkT"): qkT_out, ("A1", "vcp"): values, ("A1", "shT"): shifts,
                ("A2", "st"): exp1, ("A2", "pv"): weighed1,
                ("A2", "oT"): lambda t, b: a_out(t, "oT", O1T[:, :], MA[:, 0:NT]),
                ("A2", "x1T"): lambda t, b: a_out(t, "x1T", x1T[:, :], MA[:, 0:NT]),
                ("B", "sc"): copy_scores, ("B", "sh"): exp2,
                ("B", "pv"): lambda t, b, qt: b_out(b, f"pv{qt}", OT2[:, :], MB[:, :]),
                ("B", "ln"): keep_x2,
                ("B", "x2T"): lambda t, b: b_out(b, "x2T", x2T[:, :], MB[:, 0:NT]),
            })

            def rows_out(j, par):
                wait(act, "xgT_full", j + 1)
                wait(act, "up_full", j - 1)
                copy(xgT[:, par, :], MA[:, 0:P]).then_inc(s["xgT_ok"], 1)

            def gate(j, par):
                wait(act, "gs_ok", j + 1)
                wait(act, "act_ok", j - 1)
                a.activation(sg[:, par, :], gs[:, par, :], ACT.Sigmoid).then_inc(s["sg_ok"], 1)

            def act_out(j, par):
                wait(act, "actT_full", j + 1)
                wait(act, "down_full", j - 1)
                copy(actT[:, par, :], MB[:, :]).then_inc(s["actT_ok"], 1)

            tile_turns(act, lambda j, par: rows_out(j, par), gate, act_out)

        @block.vector
        def _(dve):
            v = nc.vector
            n = [0]
            loop = [0, 0]

            def link(ins):
                ins.then_inc(s["dchain"], 1)
                n[0] += 1
                dve.wait_ge(s["dchain"], loop[0] * loop[1] + n[0])

            def fill(t_, value):
                v.memset(t_, value)

            dve.wait_ge(s["temp_in"], 16)
            link(v.reciprocal(temp[:, :], temp[:, :]))
            link(v.tensor_scalar(trow[:, :, :], temp[:, :].unsqueeze(1).broadcast_to([P, D, H]), 1.0 / D, None, ALU.mult))
            for t_ in (QS, KS):
                link(v.memset(t_[:, :, :].rearrange("p h t -> p (h t)").bitcast(U32), 0))
            v.memset(KS[96:97, :, :], 1.0).then_inc(s["fill"], 1)
            link(v.memset(V1[:, :, :, :], 0.0))
            v.memset(V1[:, :, :, D:D + 1], 1.0).then_inc(s["fill"], 1)
            link(v.memset(ErS[:, :].bitcast(U32), 0))
            link(v.memset(er_mask[:, :], MASKED))
            dve.wait_ge(s["er_in"], 16)
            link(v.tensor_copy(er_parts[:, 0, :], er[:, :]))
            link(v.tensor_tensor(out=er_rest[:, :], in0=er[:, :], in1=er_parts[:, 0, :], op=ALU.subtract))
            link(v.tensor_copy(er_parts[:, 1, :], er_rest[:, :]))
            v.tensor_tensor(out=er_parts[:, 2, :], in0=er_rest[:, :], in1=er_parts[:, 1, :], op=ALU.subtract)\
                .then_inc(s["er_split"], 1)

            def late_constants():
                for t_ in (QZ, KZ):
                    link(v.memset(t_[:, :, :].rearrange("p h t -> p (h t)").bitcast(U32), 0))
                link(v.memset(QZ[32:64, :, :], 1.0))
                v.memset(QZ[96:128, :, :], 1.0).then_inc(s["fill"], 1)
                link(v.memset(parity[:, :], 0.0))
                link(v.memset(parity[0:64, 0:NT:2], 1.0))
                link(v.memset(parity[64:128, 1:NT:2], 1.0))
                link(v.memset(V2[:, :, :, :], 0.0))
                link(v.memset(V2[:, :, :, D:D + 1], 1.0))
                v.memset(ones_b[:, :], 1.0).then_inc(s["fill"], 1)

            def split(parts, which, whole, rest, ready):
                p = [parts[:, k, which, :] for k in range(3)]
                link(v.tensor_copy(p[0], whole))
                link(v.tensor_tensor(out=rest, in0=whole, in1=p[0], op=ALU.subtract))
                link(v.tensor_copy(p[1], rest))
                v.tensor_tensor(out=p[2], in0=rest, in1=p[1], op=ALU.subtract).then_inc(s[ready], 1)

            def layer_norm(b, r, st, mv, ve, rs, dst, ntiles, ve_ok, rs_ok, done):
                for t in range(ntiles):
                    link(v.bn_stats(st[:, t, :], r[:, t, :]))
                v.memset(pad[:, :], 0.0)
                for t in range(ntiles):
                    ins = v.bn_aggr(mv[:, t, :], st[:, t, :])
                link(ins)
                v.tensor_scalar(ve[:, :], mv[:, :, 1], LN_EPS, None, ALU.add).then_inc(s[ve_ok], 1)
                wait(dve, rs_ok, b + 1)
                for t in range(ntiles):
                    ins = v.tensor_scalar(dst[:, t, :], r[:, t, :], mv[:, t, 0:1], rs[:, t:t + 1], ALU.subtract, ALU.mult)
                ins.then_inc(s[done], 1)

            def normalise(box, rden, dst):
                link(v.reciprocal(rden, box[:, :, :, D]))
                return v.tensor_tensor(out=dst, in0=box[:, :, :, 0:D],
                                       in1=rden.unsqueeze(3).broadcast_to([P, box.shape[1], box.shape[2], D]), op=ALU.mult)

            def clamp_norms(t, b):
                wait(dve, "n2_ok", b + 1)
                v.tensor_scalar(n2c[:, :], n2[:, :], 1e-24, None, ALU.max).then_inc(s["n2c_ok"], 1)

            def scale_q_k(t, b):
                wait(dve, "rn_ok", b + 1)
                for i in range(TT):
                    v.scalar_tensor_tensor(out=qkn[:, i, 0, :, :].rearrange("p d h -> p h d"),
                                           in0=qkv[:, i, 0:C].rearrange("p (h d) -> p h d", d=D),
                                           scalar=rn[:, 2 * i:2 * i + 1],
                                           in1=trow[:, :, :].rearrange("p d h -> p h d"), op0=ALU.mult, op1=ALU.mult)
                    ins = v.tensor_scalar(qkn[:, i, 1, :, :].rearrange("p d h -> p h d"),
                                          qkv[:, i, C:2 * C].rearrange("p (h d) -> p h d", d=D),
                                          rn[:, 2 * i + 1:2 * i + 2], None, ALU.mult)
                ins.then_inc(s["qkn_ok"], 1)

            def split_q_k(t, b):
                wait(dve, "ma_free", a_full(t, "qkT"))
                wait(dve, "pa_out", b * 96)
                p = [SpA[:, k, :, :] for k in range(3)]
                link(v.tensor_copy(p[0], qkT[:, :, :]))
                link(v.tensor_tensor(out=restA[:, :, :], in0=qkT[:, :, :], in1=p[0], op=ALU.subtract))
                link(v.tensor_copy(p[1], restA[:, :, :]))
                v.tensor_tensor(out=p[2], in0=restA[:, :, :], in1=p[1], op=ALU.subtract).then_inc(s["spa_ok"], 1)
                if isinstance(t, int) and t == 0:
                    late_constants()

            def maxima(t, b, u):
                hp, qt = divmod(u, 2)
                wait(dve, "sa_full", b * 16 + u + 1)
                v.tensor_reduce(out=negm1[:, qt, 2 * hp:2 * hp + 2], in_=SA[:, u % 2, :].rearrange("p (h k) -> p h k", h=2),
                                axis=AX.X, op=ALU.max, negate=True).then_inc(s["negm1_ok"], 1)

            def norm1(t, b, pair):
                wait(dve, "ma_full", a_full(t, f"norm{pair}"))
                normalise(MA[:, :].rearrange("p (q h w) -> p q h w", q=TT, w=VW), rden1[:, :, :],
                          O1[:, :, 64 * pair:64 * pair + 64].rearrange("p q (h d) -> p q h d", d=D)).then_inc(s["ma_free"], 1)

            def residual1(t, b):
                wait(dve, "ma_full", a_full(t, "proj"))
                wait(dve, "xpb_ok", b + 1)
                v.tensor_tensor(out=res1[:, :, :], in0=MA[:, 0:NT].rearrange("p (t c) -> p t c", t=TT), in1=xpb[:, :, :],
                                op=ALU.add).then_inc(s["ma_free"], 1)

            def ln1(t, b, _):
                wait(dve, "ma_free", a_full(t, "proj"))
                layer_norm(b, res1, st1, mv1, ve1, rs1, x1, TT, "ve1_ok", "rs1_ok", "x1_ok")

            def keys2(t, b):
                wait(dve, "ma_full", a_full(t, "k2T"))
                v.tensor_scalar(qk2T[:, 1, :], MA[:, 0:NT], bk_col[:, :], None, ALU.add).then_inc(s["ma_free"], 1)
                wait(dve, "ma_free", a_full(t, "k2T"))
                split(SpB, 1, qk2T[:, 1, :], restB[:, 1, :], "spk_ok")

            def queries2(t, b):
                wait(dve, "ma_full", a_full(t, "q2T"))
                v.tensor_scalar(qk2T[:, 0, :], MA[:, 0:NT], bq_col[:, :], float(D) ** -0.5, ALU.add, ALU.mult)\
                    .then_inc(s["ma_free"], 1)
                wait(dve, "ma_free", a_full(t, "q2T"))
                split(SpB, 0, qk2T[:, 0, :], restB[:, 0, :], "spq_ok")

            def values2(t, b):
                wait(dve, "mb_full", b_full(b, "v"))
                v.tensor_tensor(out=V2[:, :, :, 0:D], in0=MB[:, 0:NT].rearrange("p (t h d) -> p t h d", t=TT, d=D),
                                in1=bv_row[:, :].rearrange("p (h d) -> p h d", d=D).unsqueeze(1).broadcast_to([P, TT, H, D]),
                                op=ALU.add).then_inc(s["mb_free"], 1)

            def stacks2(t, b):
                wait(dve, "x1_ok", b + 1)
                v.tensor_copy(x1k[:, :, :], x1[:, :, :])
                wait(dve, "kz_in", b * 32 + 32)
                v.tensor_copy(KS2[:, :, :], KZ[:, :, :])
                wait(dve, "qz_in", b * 32 + 32)
                v.tensor_tensor(out=Z[:, :, :], in0=QZ[:, :, :],
                                in1=parity[:, :].unsqueeze(1).broadcast_to([P, H, NT]), op=ALU.mult).then_inc(s["z_ok"], 1)

            def max_tiles(t, b, qb):
                if qb >= 4:
                    wait(dve, "copied", b * NQB + qb + 1)
                    v.tensor_tensor(out=Sm[:, qb % 2, :], in0=SB[:, 2 * (qb % 2) + 1, :], in1=Sb[:, qb % 2, :],
                                    op=ALU.max).then_inc(s["maxed"], 1)

            def maxima2(t, b, qb):
                wait(dve, "mb_full", b_full(b, f"tr{qb}"))
                v.tensor_reduce(out=negm2[:, qb, :], in_=MBb[:, 0:512].rearrange("p (c k) -> p c k", c=4), axis=AX.X,
                                op=ALU.max, negate=True).then_inc(s["mb_free"], 1)

            def norm2(t, b, qt):
                wait(dve, "mb_full", b_full(b, f"norm{qt}"))
                normalise(MB[:, :].rearrange("p (o h w) -> p o h w", o=1, w=VW), rden2[:, :].unsqueeze(1),
                          O2[:, qt, :].rearrange("p (o h d) -> p o h d", o=1, d=D)).then_inc(s["mb_free"], 1)

            def ln2(t, b, _):
                wait(dve, "mb_free", b_full(b, "norm1") + 1)
                link(v.tensor_tensor(out=res2[:, :, :], in0=O2[:, :, :], in1=x1k[:, :, :], op=ALU.add))
                layer_norm(b, res2, st2, mv2, ve2, rs2, x2, TT, "ve2_ok", "rs2_ok", "x2_ok")

            def add_router_bias(t, b):
                wait(dve, "mb_full", b_full(b, "logits"))
                dst = logits[:, bass.ds(b * TT, TT), :] if not isinstance(b, int) else logits[:, b * TT:(b + 1) * TT, :]
                v.tensor_tensor(out=dst, in0=MB[:, 0:TT * E].rearrange("p (t e) -> p t e", t=TT),
                                in1=rb_row[:, :].unsqueeze(1).broadcast_to([P, TT, E]), op=ALU.add).then_inc(s["mb_free"], 1)

            before_loop = [0]

            def looped(t):
                if t is not None:
                    before_loop[0] = n[0]
                    loop[:] = [t - FIRST_FULL, LINKS_A_TURN]
                else:
                    assert n[0] - before_loop[0] == LINKS_A_TURN, n[0] - before_loop[0]
                    loop[:] = [0, 0]
                    n[0] = before_loop[0] + (PAST_FULL - FIRST_FULL) * LINKS_A_TURN

            dve.sem_inc(s["mb_free"], 1)
            dve.wait_ge(s["c_in"], 16 * 5)
            turns(dve, {
                ("A1", "qkv"): clamp_norms, ("A1", "qkn"): scale_q_k, ("A1", "qkT"): split_q_k, ("A1", "d"): maxima,
                ("A2", "nm"): norm1, ("A2", "proj"): residual1, ("A2", "ln"): ln1, ("A2", "k2T"): keys2, ("A2", "q2T"): queries2,
                ("B", "v"): values2, ("B", "build"): stacks2, ("B", "sc"): max_tiles, ("B", "tr"): maxima2, ("B", "nm"): norm2,
                ("B", "ln"): ln2, ("B", "lg"): add_router_bias,
            }, looped)

            def bc(ap, axis, shape):
                return ap.unsqueeze(axis).broadcast_to(shape)

            dve.wait_ge(s["mb_free"], b_full(NB - 1, "logits") + 1)
            dve.wait_ge(s["consts"], 2)
            TE = [P, NTK, E]
            link(v.tensor_reduce(out=mx[:, :], in_=logits[:, :, :], axis=AX.X, op=ALU.max))
            link(v.tensor_tensor(out=eq[:, :, :], in0=logits[:, :, :], in1=bc(mx[:, :], 2, TE), op=ALU.is_ge))
            link(v.tensor_tensor(out=cand[:, :, :], in0=eq[:, :, :], in1=bc(iota_e[:, :], 1, TE), op=ALU.mult))
            link(v.tensor_reduce(out=first[:, :], in_=cand[:, :, :], axis=AX.X, op=ALU.min))
            link(v.tensor_tensor(out=oh[:, :, :], in0=bc(iota_e[:, :], 1, TE), in1=bc(first[:, :], 2, TE), op=ALU.is_equal))
            v.tensor_copy(ohb[:, :, :], oh[:, :, :]).then_inc(s["oh_ok"], 1)
            dve.wait_ge(s["ranked"], 1)
            link(v.tensor_copy(cnt[:, :], MA[:, 64:64 + E]))
            link(v.tensor_tensor(out=gt[:, :, :], in0=bc(cnt[:, :], 2, [P, E, NTK]), in1=bc(iota_c[:, :], 1, [P, E, NTK]), op=ALU.is_gt))
            link(v.tensor_reduce(out=nti[:, :], in_=gt[:, :, :], axis=AX.X, op=ALU.add))
            link(v.tensor_copy(ends[:, :], nti[:, :]))
            for e in range(1, E):
                link(v.tensor_tensor(out=ends[:, e:e + 1], in0=ends[:, e:e + 1], in1=ends[:, e - 1:e], op=ALU.add))
            link(v.tensor_tensor(out=base[:, :], in0=ends[:, :], in1=nti[:, :], op=ALU.subtract))
            link(v.tensor_scalar(base[:, :], base[:, :], float(SLOTS), None, ALU.mult))
            link(v.tensor_tensor(out=pos[:, :, :], in0=MA[:, 0:64].rearrange("p (t e) -> p t e", e=E), in1=bc(base[:, :], 1, TE), op=ALU.add))
            link(v.tensor_tensor(out=pos[:, :, :], in0=pos[:, :, :], in1=oh[:, :, :], op=ALU.mult))
            link(v.tensor_reduce(out=slotf[:, :], in_=pos[:, :, :], axis=AX.X, op=ALU.add))
            v.tensor_copy(slot[:, :], slotf[:, :]).then_inc(s["slot_ok"], 1)
            link(v.tensor_tensor(out=le[:, :, :], in0=bc(ends[:, :], 1, [P, NTILE, E]), in1=bc(iota_t[:, :], 2, [P, NTILE, E]), op=ALU.is_le))
            link(v.tensor_reduce(out=tef[:, :], in_=le[:, :, :], axis=AX.X, op=ALU.add))
            v.tensor_scalar(tile_e[:, :], tef[:, :], float(E - 1), None, ALU.min).then_inc(s["te_ok"], 1)

            def glu(j, par):
                wait(dve, "up_full", j + 1)
                wait(dve, f"bt_in{par}", of_parity(j, par, 32))
                v.tensor_tensor(out=gs[:, par, :], in0=UP[par][1], in1=b1t[:, par, F:2 * F], op=ALU.add).then_inc(s["gs_ok"], 1)
                v.tensor_tensor(out=aa[:, par, :], in0=UP[par][0], in1=b1t[:, par, 0:F], op=ALU.add).then_inc(s["aa_ok"], 1)
                wait(dve, "aa_ok", j + 1)
                wait(dve, "sg_ok", j + 1)
                v.tensor_tensor(out=act_[:, par, :], in0=aa[:, par, :], in1=sg[:, par, :], op=ALU.mult).then_inc(s["act_ok"], 1)

            def add_b2(j, par):
                wait(dve, "down_full", j + 1)
                wait(dve, f"y_out{par}", of_parity(j, par, 16) - 16)
                v.tensor_tensor(out=y[:, par, :], in0=SB[:, 2 + par, 0:C], in1=b2t[:, par, :], op=ALU.add).then_inc(s["y_ok"], 1)

            tile_turns(dve, None, glu, add_b2)
            dve.wait_ge(s["gath"], 16 * NTK)
            link(v.tensor_tensor(out=res3[:, :, :], in0=x2all[:, :, :], in1=yg[:, :, :], op=ALU.add))
            layer_norm(0, res3, st3, mv3, ve3, rs3, x3, NTK, "ve3_ok", "rs3_ok", "x3_ok")

        @block.tensor
        def _(pe):
            mm = nc.tensor.matmul

            def tr(dst, src, idn):
                return nc.tensor.transpose(dst, src, idn)

            def a_box(t, use):
                wait(pe, "ma_free", a_full(t, use) - 1)

            def b_box(b, use):
                wait(pe, "mb_free", b_full(b, use))

            def project_x(t, b):
                wait(pe, "xT_in", b * 16 + 16)
                for i in range(TT):
                    a_box(t, f"qkv{i}")
                    mm(MA[:, 0:3 * C], xT[:, i * P:(i + 1) * P], wqkv[:, :], start=True, stop=True).then_inc(s["ma_full"], 1)

            def transpose_q_k(t, b):
                wait(pe, "qkn_ok", b + 1)
                a_box(t, "qkT")
                for w in range(2):
                    for i in range(TT):
                        last = tr(MA[:, w * NT + i * P:w * NT + (i + 1) * P], qkn[:, i, w, :, :].rearrange("p d h -> p (d h)"), ident[:, :])
                last.then_inc(s["ma_full"], 1)

            def scores1(t, b, u):
                hp, qt = divmod(u, 2)
                if u == 0:
                    wait(pe, "qs_in", b * 32 + 32)
                if u < 2:
                    wait(pe, "exp1", b * 8)
                else:
                    wait(pe, "negm1_ok", b * 16 + u - 1)
                for i in range(2):
                    h = 2 * hp + i
                    last = mm(SA[:, u % 2, i * NT:(i + 1) * NT], QS[0:96, h, qt * P:(qt + 1) * P], KS[0:96, h, :], start=True, stop=True)
                last.then_inc(s["sa_full"], 1)

            def transpose_shifts(t, b):
                wait(pe, "negm1_ok", b * 16 + 16)
                a_box(t, "shiftT")
                tr(MAb[0:TT * H, 0:P], negm1[:, :, :].rearrange("p q h -> p (q h)"), identb[:, :]).then_inc(s["ma_full"], 1)

            def scores_t(t, b, u):
                if u == 0:
                    wait(pe, "m_in", b * 16 + 16)
                    wait(pe, "negm1_ok", b * 16 + 16)
                else:
                    wait(pe, "exp1", b * 8 + u)
                for kt in range(TT):
                    for i in range(2):
                        h = 2 * u + i
                        last = mm(SA[:, kt, i * NT:(i + 1) * NT], KS[:, h, kt * P:(kt + 1) * P], QS[:, h, :], start=True, stop=True)
                last.then_inc(s["st_full"], 1)

            def weigh1(t, b, grp):
                if grp == 0:
                    wait(pe, "v1_ok", b + 1)
                wait(pe, "exp1", b * 8 + 2 * grp + 2)
                if grp % 2 == 0:
                    a_box(t, f"pv{grp // 2}")
                for kt in range(TT):
                    for i in range(HEADS_A_GROUP):
                        h = grp * HEADS_A_GROUP + i
                        last = mm(MA[VW * i:VW * i + VW, (grp % 2) * NT:(grp % 2 + 1) * NT], V1[:, kt, h, :],
                                  P1[:, grp % 2, kt, i, :], start=(kt == 0), stop=(kt == TT - 1))
                if grp % 2:
                    last.then_inc(s["ma_full"], 1)

            def transpose_o(t, b, pair):
                a_box(t, f"norm{pair}")
                for qt in range(TT):
                    for g2 in range(2):
                        last = tr(MA[:, qt * 256 + g2 * P:qt * 256 + (g2 + 1) * P],
                                  OT1[:, g2 * NT + qt * P:g2 * NT + (qt + 1) * P], ident[:, :])
                last.then_inc(s["ma_full"], 1)

            def transpose_rows(src):
                for i in range(TT):
                    last = tr(MA[:, i * P:(i + 1) * P], src[:, i, :], ident[:, :])
                return last

            def o_to_cols(t, b):
                a_box(t, "oT")
                transpose_rows(O1).then_inc(s["ma_full"], 1)

            def project_o(t, b):
                a_box(t, "proj")
                for i in range(TT):
                    last = mm(MA[:, i * C:(i + 1) * C], O1T[:, i * P:(i + 1) * P], wproj[:, :], start=True, stop=True)
                last.then_inc(s["ma_full"], 1)

            def x1_to_cols(t, b):
                wait(pe, "x1_ok", b + 1)
                a_box(t, "x1T")
                transpose_rows(x1).then_inc(s["ma_full"], 1)

            def project_q2(t, b):
                a_box(t, "q2T")
                mm(MA[:, 0:NT], wq[:, :], x1T[:, :], start=True, stop=True).then_inc(s["ma_full"], 1)

            def project_k2(t, b):
                wait(pe, "cT_in", b * 16 + 16)
                a_box(t, "k2T")
                mm(MA[:, 0:NT], wk[:, :], cT[:, :], start=True, stop=True).then_inc(s["ma_full"], 1)

            def project_v2(t, b):
                b_box(b, "v")
                for i in range(TT):
                    last = mm(MB[:, i * C:(i + 1) * C], cT[:, i * P:(i + 1) * P], wv[:, :], start=True, stop=True)
                last.then_inc(s["mb_full"], 1)

            def scores2(t, b, qb):
                if qb == 0:
                    wait(pe, "z_ok", b + 1)
                if qb >= 2:
                    wait(pe, "exp2", b * NQB + qb - 1)
                for kt in range(1 if qb < 4 else 2):
                    bank = SB[:, 2 * (qb % 2) + kt, :].rearrange("p (h q) -> p h q", h=H)
                    for h in range(H):
                        mm(bank[:, h, :], KS2[:, h, kt * P:(kt + 1) * P], Z[:, h, QB * qb:QB * (qb + 1)],
                           start=(h == 0), stop=False, skip_group_check=True)
                    for q in range(0, QB, 2):
                        w = NT - 1 - (QB * qb + q) + kt * P
                        last = mm(bank[:, :, q:q + 2], ErS[:, w:w + P], Z[:, :, QB * qb + q:QB * qb + q + 2],
                                  start=False, stop=False, skip_group_check=True)
                last.then_inc(s["sc_full"], 1)

            def transpose_scores(t, b, qb):
                if qb < 4:
                    wait(pe, "copied", b * NQB + qb + 1)
                else:
                    wait(pe, "maxed", b * 4 + qb - 3)
                src = Sb if qb < 4 else Sm
                b_box(b, f"tr{qb}")
                for c in range(4):
                    last = tr(MBb[:, c * P:(c + 1) * P], src[:, qb % 2, c * P:(c + 1) * P], identb[:, :])
                last.then_inc(s["mb_full"], 1)

            def shift(t, b, qb):
                wait(pe, "mb_free", b_full(b, f"tr{qb}") + 1)
                for kt in range(1 if qb < 4 else 2):
                    for c in range(4):
                        last = mm(SB[:, 2 * (qb % 2) + kt, c * P:(c + 1) * P], negm2[:, qb, c:c + 1].broadcast_to([P, P]),
                                  identb[:, :], start=False, stop=True, skip_group_check=True)
                last.then_inc(s["shifted"], 1)

            def weigh2(t, b, qt):
                wait(pe, "exp2", b * NQB + 4 * qt + 4)
                b_box(b, f"pv{qt}")
                for grp in range(NG):
                    for kt in range(qt + 1):
                        for i in range(HEADS_A_GROUP):
                            h = grp * HEADS_A_GROUP + i
                            rhs = P2a[:, h, :] if qt == 0 else P2b[:, kt, h, :]
                            last = mm(MB[VW * i:VW * i + VW, grp * P:(grp + 1) * P], V2[:, kt, h, :], rhs,
                                      start=(kt == 0), stop=(kt == qt))
                last.then_inc(s["mb_full"], 1)

            def transpose_o2(t, b, qt):
                b_box(b, f"norm{qt}")
                for grp in range(NG):
                    last = tr(MB[:, grp * P:(grp + 1) * P], OT2[:, grp * P:(grp + 1) * P], ident[:, :])
                last.then_inc(s["mb_full"], 1)

            def x2_to_cols(t, b):
                wait(pe, "x2_ok", b + 1)
                b_box(b, "x2T")
                for i in range(TT):
                    last = tr(MB[:, i * P:(i + 1) * P], x2[:, i, :], ident[:, :])
                last.then_inc(s["mb_full"], 1)

            def router(t, b):
                b_box(b, "logits")
                for i in range(TT):
                    last = mm(MB[:, i * E:(i + 1) * E], x2T[:, i * P:(i + 1) * P], wr[:, :], start=True, stop=True)
                last.then_inc(s["mb_full"], 1)

            pe.wait_ge(s["ident_ok"], 1)
            pe.wait_ge(s["consts"], 1)
            pe.wait_ge(s["wqkv_in"], 16)

            def first_weights(t, b):
                if isinstance(t, int) and t == 0:
                    pe.wait_ge(s["w_in"], 16 * 5)
                    pe.wait_ge(s["fill"], 4)
                    pe.wait_ge(s["er_stacked"], 16 * 14)

            turns(pe, {
                ("A1", "qkv"): project_x, ("A1", "qkT"): transpose_q_k, ("A1", "d"): scores1, ("A1", "shT"): transpose_shifts,
                ("A1", "vcp"): first_weights,
                ("A2", "st"): scores_t, ("A2", "pv"): weigh1, ("A2", "nm"): transpose_o, ("A2", "oT"): o_to_cols,
                ("A2", "proj"): project_o, ("A2", "x1T"): x1_to_cols, ("A2", "q2T"): project_q2, ("A2", "k2T"): project_k2,
                ("B", "v"): project_v2, ("B", "sc"): scores2, ("B", "tr"): transpose_scores, ("B", "sh"): shift,
                ("B", "pv"): weigh2, ("B", "nm"): transpose_o2, ("B", "x2T"): x2_to_cols, ("B", "lg"): router,
            })
            pe.wait_ge(s["oh_ok"], 1)
            mm(MA[:, 0:NTK * E], before[:, :], ohb[:, :, :].rearrange("p t e -> p (t e)"), start=True, stop=False, skip_group_check=True)
            for t in range(NTK):
                for u in range(t + 1, NTK):
                    mm(MA[:, u * E:(u + 1) * E], ones_b[:, :], ohb[:, t, :], start=False, stop=False, skip_group_check=True)
                last = mm(MA[:, NTK * E:NTK * E + E], ones_b[:, :], ohb[:, t, :], start=False, stop=(t == NTK - 1), skip_group_check=True)
            last.then_inc(s["ranked"], 1)
            pe.wait_ge(s["te_ok"], 1)
            pe.wait_ge(s["bigw"], 32)

            def rows_to_cols(j, par):
                wait(pe, f"xg_in{par}", of_parity(j, par, 16))
                wait(pe, "xgT_ok", j)
                tr(MA[:, 0:P], xg[:, par, :], ident[:, :]).then_inc(s["xgT_full"], 1)

            def up(j, par):
                e = pe.value_load(tile_e[0:1, bass.ds(j, 1)], min_val=0, max_val=E - 1)
                wait(pe, "xgT_ok", j + 1)
                wait(pe, "aa_ok", j - 1)
                for k in (1, 0):
                    last = mm(UP[par][k], xgT[:, par, :], w1_sb[:, bass.ds(e, 1), k * F:(k + 1) * F].rearrange("p o f -> p (o f)"), start=True, stop=True)
                last.then_inc(s["up_full"], 1)

            def down(j, par):
                e = pe.value_load(tile_e[0:1, bass.ds(j, 1)], min_val=0, max_val=E - 1)
                wait(pe, "act_ok", j + 1)
                wait(pe, "actT_ok", j)
                for k in range(F // P):
                    last = tr(MB[:, k * P:(k + 1) * P], act_[:, par, k * P:(k + 1) * P], ident[:, :])
                last.then_inc(s["actT_full"], 1)
                wait(pe, "actT_ok", j + 1)
                wait(pe, "y_ok", j - 1)
                for k in range(F // P):
                    last = mm(SB[:, 2 + par, 0:C], actT[:, par, k * P:(k + 1) * P], w2_sb[:, bass.ds(e, 1), k, :].rearrange("p o c -> p (o c)"), start=(k == 0), stop=(k == F // P - 1))
                last.then_inc(s["down_full"], 1)

            tile_turns(pe, rows_to_cols, up, down)


def kernel(**inputs):
    import numpy as np
    import concourse.bacc as bacc
    from concourse.bass_utils import run_bass_kernel_spmd as run

    def cols(a):
        return np.asarray(a).transpose(0, 2, 1)

    def by_part(w):
        w = np.asarray(w)
        return w.reshape((H, D) + w.shape[1:]).swapaxes(0, 1).reshape(w.shape)

    i = {k: np.asarray(v) for k, v in inputs.items()}
    arrays = {
        "x_rows": i["x"].reshape(NB, TT, P, C).transpose(0, 2, 1, 3),
        "x_cols": cols(i["x"]),
        "ctx_cols": cols(i["ctx_1024"]),
        "wqkv_t": i["L0_attn_qkv_w"].T,
        "temperature": i["L0_attn_temperature"].reshape(H),
        "wproj_t": i["L0_attn_proj_w"].T,
        "proj_b": i["L0_attn_proj_b"],
        "wq_t": by_part(i["L0_xattn_Wq"]).T,
        "bq": by_part(i["L0_xattn_bq"]),
        "wk_t": by_part(i["L0_xattn_Wk"]).T,
        "bk": by_part(i["L0_xattn_bk"]),
        "wv_t": i["L0_xattn_Wv"].T,
        "bv": i["L0_xattn_bv"],
        "er_t": i["L0_xattn_Er"].T,
        "router_w": i["L0_ffn_router_w"],
        "router_b": i["L0_ffn_router_b"],
        "w1": i["L0_ffn_w1"],
        "b1": i["L0_ffn_b1"],
        "w2": i["L0_ffn_w2"],
        "b2": i["L0_ffn_b2"],
    }
    arrays = {k: np.ascontiguousarray(v) for k, v in arrays.items()}
    nc = bacc.Bacc("TRN2", target_bir_lowering=False, num_devices=1)
    args = [nc.dram_tensor("in_" + k, a.shape, FP32, kind="ExternalInput").ap() for k, a in arrays.items()]
    out = nc.dram_tensor("out", (NB, NT, C), FP32, kind="ExternalOutput").ap()
    build(nc, *args, out)
    r = run(nc, [{"in_" + k: a for k, a in arrays.items()}], core_ids=[0])
    return r.results[0]["out"]
```

```python
from contextlib import ExitStack

import concourse.bass as bass
from concourse import mybir

FP32 = mybir.dt.float32
BF16 = mybir.dt.bfloat16
I32 = mybir.dt.int32
U32 = mybir.dt.uint32
ALU = mybir.AluOpType
ACT = mybir.ActivationFunctionType
AX = mybir.AxisListType

LINKS_A_TURN = 30
NB, NT, C = 4, 256, 128
H, D = 16, 8
P = 128
TT = NT // P
NTK = NB * TT
HEADS_A_GROUP = 4
NG = H // HEADS_A_GROUP
VW = 32
NTERM = 6
SR = NTERM * D
QB = 32
NQB = NT // QB
E, F = 8, 512
SLOTS = P
NTILE = NB * TT + E - 1
LN_EPS = 1e-5
MASKED = -1e30
ROW = C + 1
REGION = NB * NT
PARKED = NTILE - E
BLANK_PIECES = 8
WARMING = 18
ABIAS = 2 * F + C



def steps_of(text):
    return tuple(x.split(".") for x in text.split())


FIRST = steps_of("""
    A1.qkv A1.qkn A1.qkT A1.k2 A1.qsin A1.d0 A1.d1 A1.d2 A1.d3 A1.d4 A1.d5 A1.d6 A1.d7 A1.k4 A1.d8 A1.d9
    A1.d10 A1.d11 A1.d12 A1.vcp A1.d13 A1.d14 A1.d15 A1.shT
""")
SECOND = steps_of("""
    A1.qkv A2.st0 A1.k1 A1.qkn A2.st1 A1.qkT A2.st2 A2.st3 A2.st4 A2.k2T A2.st5 A2.st6 A2.st7 A2.pv0 A2.pv1
    A2.st8 A1.k5 A2.st9 A2.st10 A2.st11 A2.nm0 A2.st12 A2.st13 A2.pv2 A2.st14 A2.st15 A1.k3 A1.qsin A2.pv3
    A2.kc A2.xpb A2.nm1 A1.d0 A1.d1 A1.d2 A2.oT A1.d3 A1.d4 A2.proj A2.ln1 A1.d5 A1.vcp A1.d6 A1.k0 A1.d7
    A2.x1T A1.d8 A1.d9 A1.d10 A1.d11 A1.d12 A2.q2T A1.d13 A1.d14 A1.d15 A1.shT
""")
FULL = steps_of("""
    B.build A1.qkv B.sc0 B.sc1 B.tr0 A2.st0 A2.st1 B.sh0 A1.qkn A2.st2 B.tr1 A2.st3 A2.xpb B.sc2 A2.st4
    B.sh1 B.v A2.st5 A2.pv0 A2.st6 B.tr2 A2.st7 B.sc3 A2.pv1 B.rest B.sh2 B.tr3 A1.qkT A2.st8 B.sc4 B.sh3
    A2.st9 A2.st10 B.sc5 A2.st11 B.tr4 A2.st12 A2.st13 A2.nm0 A2.st14 B.tr5 A2.st15 A1.qsin B.sh4 B.pv0
    A2.k2T B.sc6 A2.pv2 A1.d0 A1.d1 A2.pv3 A1.d2 A1.d3 B.sh5 A1.d4 A2.nm1 B.tr6 A1.d5 A1.d6 B.sc7 A1.d7
    A1.d8 A2.oT A2.proj B.tr7 A1.vcp B.sh6 B.sh7 A2.ln1 A1.d9 B.nm0 A1.d10 A2.x1T A2.q2T B.pv1 A1.d11 A1.d12
    B.nm1 A1.d13 B.ln2 A1.d14 A1.d15 B.x2T B.lg A2.kc A1.shT B.rk
""")
LAST_BUT_ONE = steps_of("""
    A2.st0 A2.st1 B.build B.sc0 A2.st2 A2.st3 B.rest B.sc1 B.tr0 A2.st4 A2.st5 A2.pv0 B.sh0 A2.st6 B.tr1
    A2.st7 B.sc2 B.sh1 A2.pv1 B.tr2 A2.st8 B.sc3 B.sh2 B.v A2.st9 A2.st10 B.tr3 B.sc4 A2.st11 B.sh3 A2.nm0
    B.tr4 A2.st12 A2.k2T A2.xpb B.sc5 B.sh4 B.pv0 A2.st13 A2.st14 B.tr5 B.sc6 B.sh5 A2.pv2 A2.st15 B.tr6
    B.sc7 A2.pv3 B.nm0 A2.nm1 B.tr7 B.sh6 A2.oT B.sh7 A2.kc A2.proj B.pv1 A2.ln1 A2.x1T B.nm1 A2.q2T B.ln2
    B.x2T B.lg B.rk
""")
LAST = steps_of("""
    B.build B.v B.rest B.sc0 B.tr0 B.sc1 B.sh0 B.tr1 B.sc2 B.sh1 B.tr2 B.sc3 B.sh2 B.tr3 B.sc4 B.sh3 B.tr4
    B.sc5 B.sh4 B.tr5 B.sc6 B.sh5 B.tr6 B.sc7 B.pv0 B.sh6 B.tr7 B.sh7 B.nm0 B.pv1 B.nm1 B.ln2 B.x2T B.lg
    B.rk
""")
TURNS = NB + 2
FIRST_FULL, PAST_FULL = 2, NB
ORDERS = {0: FIRST, 1: SECOND, TURNS - 2: LAST_BUT_ONE, TURNS - 1: LAST}

A_FILLS = {"A1.qkv": ("qkv0", "qkv1"), "A1.qkT": ("qkT",), "A2.pv1": ("pv0",), "A2.nm0": ("norm0",), "A2.k2T": ("k2T",),
           "A2.pv3": ("pv1",), "A2.nm1": ("norm1",), "A2.oT": ("oT",), "A2.proj": ("proj",), "A2.x1T": ("x1T",),
           "A2.q2T": ("q2T",), "A1.shT": ("shiftT",)}
B_FILLS = {"B.v": ("v",), **{f"B.tr{q}": (f"tr{q}",) for q in range(NQB)}, "B.pv0": ("pv0",), "B.pv1": ("pv1",),
           "B.nm0": ("norm0",), "B.nm1": ("norm1",), "B.x2T": ("x2T",), "B.lg": ("logits",), "B.rk": ("ranks",)}


def order(t):
    return ORDERS.get(t, FULL) if isinstance(t, int) else FULL


def fills(table, t):
    return [f for stage, step in order(t) for f in table.get(f"{stage}.{step}", ())]


def a_full(t, use):
    first, full = len(fills(A_FILLS, 0)), len(fills(A_FILLS, FIRST_FULL))
    before = 0 if isinstance(t, int) and t == 0 else first + (t - 1) * full
    return before + fills(A_FILLS, t).index(use) + 1


def b_full(b, use):
    in_order = fills(B_FILLS, b + 2)
    return b * len(in_order) + in_order.index(use) + 1


def build(nc, x_rows, x_cols, ctx_cols, wqkv_t, temperature, wproj_t, proj_b, wq_t, bq, wk_t, bk, wv_t, bv,
          er_t, router_w, router_b, w1, b1, w2, b2, out):
    ctx = ExitStack()
    with ctx:
        def one(ap):
            return ap.squeeze(0)

        def sb(name, shape, dt=FP32):
            return ctx.enter_context(nc.sbuf_tensor(name, shape, dt))

        def pb(name, shape, dt=FP32):
            return ctx.enter_context(nc.psum_tensor(name, shape, dt))

        def sem(name):
            return ctx.enter_context(nc.semaphore(name))

        def dram(name, shape, dt=FP32):
            return nc.dram_tensor(name, shape, dt, kind="Internal").ap()

        parts_a = dram("parts_a", (2, NTERM, P, NT), BF16)
        parts_b = dram("parts_b", (2, NTERM, P, NT), BF16)
        shift_a = dram("shift_a", (NB, TT, H, P), BF16)
        sorted_x = dram("sorted_x", (E * REGION + PARKED * SLOTS, ROW))
        bias_parts = dram("bias_parts", (3, E, ABIAS), BF16)

        ident = sb("ident", [P, P])
        identb = sb("identb", [P, P], BF16)
        ones_b = sb("ones_b", [P, P], BF16)
        ones_3 = sb("ones_3", [P, P], BF16)
        before = sb("before", [P, P], BF16)
        parity = sb("parity", [P, NT], BF16)
        pad = sb("pad", [P, 1])
        carrier = sb("carrier", [P, 2])
        early = sb("early", [P, 1])
        half = sb("half", [P, NTK])
        wqkv = sb("wqkv", [P, 3 * C])
        wproj = sb("wproj", [P, C])
        wq = sb("wq", [P, C])
        wk = sb("wk", [P, C])
        wv = sb("wv", [P, C])
        wr = sb("wr", [P, E])
        pbias = sb("pbias", [P, C])
        bv_row = sb("bv_row", [P, C])
        rb_row = sb("rb_row", [P, E])
        bq_col = sb("bq_col", [P, 1])
        bk_col = sb("bk_col", [P, 1])
        temp = sb("temp", [P, H])
        trow = sb("trow", [P, D, H])
        er_parts = sb("er_parts", [D, 3, NT], BF16)
        er_mask = sb("er_mask", [1, 2 * NT], BF16)
        EW = 400
        ErS = sb("ErS", [P, EW], BF16)
        w1_sb = sb("w1_sb", [P, E, 2 * F])
        w2_sb = sb("w2_sb", [P, E, F // P, C])

        xT = sb("xT", [P, NT])
        x_tok = sb("x_tok", [P, TT, C])
        xpb = sb("xpb", [P, TT, C])
        qkv = sb("qkv", [P, TT, 3 * C])
        sq = sb("sq", [P, 4, C], BF16)
        n2 = sb("n2", [P, 4])
        n2c = sb("n2c", [P, 4])
        rn = sb("rn", [P, 4])
        qkn = sb("qkn", [P, TT, 2, D, H])
        qkT = sb("qkT", [P, 2, NT])
        restA = sb("restA", [P, 2, NT])
        SpA = sb("SpA", [P, 3, 2, NT], BF16)
        V1 = sb("V1", [P, TT, H, VW])
        QS = sb("QS", [P, H, NT], BF16)
        KS = sb("KS", [P, H, NT], BF16)
        negm1 = sb("negm1", [P, TT, H], BF16)
        nmT = sb("nmT", [TT * H, P], BF16)
        P1 = sb("P1", [P, 2, TT, HEADS_A_GROUP, NT])
        OT1 = sb("OT1", [P, 2 * NT])
        rden1 = sb("rden1", [P, TT, 2 * HEADS_A_GROUP])
        O1 = sb("O1", [P, TT, C])
        O1T = sb("O1T", [P, NT])
        res1 = sb("res1", [P, TT, C])
        st1 = sb("st1", [P, TT, 6])
        mv1 = sb("mv1", [P, TT, 2])
        ve1 = sb("ve1", [P, TT])
        rs1 = sb("rs1", [P, TT])
        x1 = sb("x1", [P, TT, C])
        x1T = sb("x1T", [P, NT])
        x1k = sb("x1k", [P, TT, C])

        cT = sb("cT", [P, NT])
        qk2T = sb("qk2T", [P, 2, NT])
        restB = sb("restB", [P, 2, NT])
        SpB = sb("SpB", [P, 3, 2, NT], BF16)
        V2 = sb("V2", [P, TT, H, VW])
        QZ = sb("QZ", [P, H, NT], BF16)
        KZ = sb("KZ", [P, H, NT], BF16)
        Z = sb("Z", [P, H, NT], BF16)
        KS2 = sb("KS2", [P, H, NT], BF16)
        Sb = sb("Sb", [P, 2, 512], BF16)
        Sm = sb("Sm", [P, 2, 512], BF16)
        negm2 = sb("negm2", [P, NQB, 4], BF16)
        P2a = sb("P2a", [P, H, P])
        P2b = sb("P2b", [P, 2, H, P])
        er = P2a[0:D, 0:2, :].rearrange("d h q -> d (h q)")
        er_rest = P2a[0:D, 2:4, :].rearrange("d h q -> d (h q)")
        OT2 = sb("OT2", [P, 512])
        rden2 = sb("rden2", [P, H])
        O2 = sb("O2", [P, TT, C])
        res2 = sb("res2", [P, TT, C])
        st2 = sb("st2", [P, TT, 6])
        mv2 = sb("mv2", [P, TT, 2])
        ve2 = sb("ve2", [P, TT])
        rs2 = sb("rs2", [P, TT])
        x2 = sb("x2", [P, TT, ROW])
        x2T = sb("x2T", [P, NT])
        logits = sb("logits", [P, TT, E])

        iota_e = sb("iota_e", [P, E])
        iota_t = sb("iota_t", [P, NTILE])
        iota_c = sb("iota_c", [P, NTK])
        expert_row = sb("expert_row", [P, E])
        mx = sb("mx", [P, TT])
        eq = sb("eq", [P, TT, E])
        cand = sb("cand", [P, TT, E])
        first = sb("first", [P, TT])
        oh = sb("oh", [P, TT, E])
        ohb = sb("ohb", [P, TT, E], BF16)
        cnt = sb("cnt", [P, E])
        start = sb("start", [P, E])
        gt = sb("gt", [P, E, NTK])
        sums = [sb(f"sums{k}", [P, E // 2 + E]) for k in range(4)]
        nti, ends = sums[0][:, E // 2:], sums[3][:, E // 2:]
        skip = sb("skip", [P, E])
        pos = sb("pos", [P, TT, E])
        mine = sb("mine", [P, TT, E])
        slotf = sb("slotf", [P, TT])
        slot = sb("slot", [P, TT], I32)
        le = sb("le", [P, NTILE, E])
        skips = sb("skips", [P, NTILE, E])
        tef = sb("tef", [P, NTILE])
        tile_e = sb("tile_e", [P, NTILE], I32)
        skipped = sb("skipped", [P, NTILE])
        tile_row = sb("tile_row", [P, NTILE], I32)
        blank = sb("blank", [P, ROW])

        QZr = QZ[:, :, :].rearrange("p h t -> p (h t)").bitcast(FP32)
        KZr = KZ[:, :, :].rearrange("p h t -> p (h t)").bitcast(FP32)
        def rooms(tile, spec):
            at, got = 0, []
            for n_, width in spec:
                got.append(tile[:, at:at + n_ * width].rearrange("p (n w) -> p n w", w=width))
                at += n_ * width
            return got

        flatP1 = P1[:, :, :, :, :].rearrange("p g k h q -> p (g k h q)")
        flatP2b = P2b[:, :, :, :].rearrange("p k h q -> p (k h q)")
        brow, brest = flatP2b[0:E, 0:ABIAS], flatP2b[0:E, ABIAS:2 * ABIAS]
        bparts = flatP2b[0:E, 2 * ABIAS:2 * ABIAS + 3 * ABIAS // 2].bitcast(BF16).rearrange("e (w f) -> e w f", w=3)
        value_bias, gate_bias = QS[:, :, :].rearrange("p h t -> p (h t)"), KS[:, :, :].rearrange("p h t -> p (h t)")
        down_bias = SpA[:, :, :, :].rearrange("p k w t -> p (k w t)")
        xg, = rooms(KZr, ((NTILE, ROW),))
        act_, xgT, y, res3, row = rooms(flatP1, ((2, F), (2, P), (2, C), (2, C), (2, C)))
        sg, actT = rooms(P2a[:, :, :].rearrange("p h q -> p (h q)"), ((2, F), (2, F)))
        st3 = sb("st3", [P, 2, 6])
        mv3 = sb("mv3", [P, 2, 2])
        ve3 = sb("ve3", [P, 2])
        rs3 = sb("rs3", [P, 2])
        token = sb("token", [P, 2], I32)

        SA = pb("SA", [P, 2, 512])
        MA = pb("MA", [P, 512])
        SB = pb("SB", [P, 4, 512])
        MB = pb("MB", [P, 512])
        MAb = MA[:, :].bitcast(BF16)
        MBb = MB[:, :].bitcast(BF16)
        UP = ([SA[:, 0, :], SA[:, 1, :]], [SB[:, 0, :], SB[:, 1, :]])

        s = {n: sem(n) for n in (
            "wqkv_in", "w_in", "temp_in", "c_in", "er_in", "fill", "v1_fill", "staging_fill", "ident_ok", "consts", "er_split", "er_stacked", "bigw",
            "dchain", "pchain",
            "ma_full", "ma_free", "mb_full", "mb_free",
            "xT_in", "xtok_in", "n2_ok", "n2c_ok", "rn_ok", "qkn_ok", "v1_ok", "xpb_ok", "spa_ok", "pa_out", "qs_in",
            "sa_full", "negm1_ok", "m_out", "m_in", "st_full", "exp1", "ve1_ok", "rs1_ok", "x1_ok",
            "cT_in", "spk_ok", "spq_ok", "pk_out", "pq_out", "kz_in", "qz_in", "z_ok", "sc_full", "copied", "maxed", "shifted",
            "exp2", "ve2_ok", "rs2_ok", "x2_ok",
            "oh_ok", "slot_ok", "te_ok", "row_known", "scat", "bias_in", "bias_split", "bias_out", "bias_back", "xg_in0", "xg_in1", "xg_in2", "xg_in3", "row_ok", "xgT_full", "xgT_ok", "gate_full", "up_full",
            "sg_ok", "act_ok", "actT_full", "actT_ok", "down_full", "res3_ok", "st3_ok", "mv3_ok",
            "ve3_ok", "rs3_ok", "x3_ok", "o_out0", "o_out1",
        )}
        block = ctx.enter_context(nc.Block())

        def scattered(b):
            return 16 * BLANK_PIECES + 16 * TT * b

        def wait(eng, name, value):
            if not (isinstance(value, int) and value <= 0):
                eng.wait_ge(s[name], value)

        def turns(eng, steps, looped=None):
            def turn(t):
                batch = {"A1": t, "A2": t - 1, "B": t - 2}
                for stage, step in order(t):
                    name, index = step.rstrip("0123456789"), step[len(step.rstrip("0123456789")):]
                    if (stage, name) in steps:
                        steps[stage, name](t, batch[stage], *([int(index)] if index else []))

            for t in range(FIRST_FULL):
                turn(t)
            with eng.Fori(FIRST_FULL, PAST_FULL) as t:
                if looped:
                    looped(t)
                turn(t)
            if looped:
                looped(None)
            for t in range(PAST_FULL, TURNS):
                turn(t)

        def tile_steps(eng, *work):
            def step(j, par):
                for offset, f in work:
                    if not isinstance(j, int) or 0 <= j + offset < NTILE:
                        f(j + offset, (par + offset) % 2)

            first, past = 4, NTILE - 3
            for j in range(-2, first):
                step(j, j % 2)
            with eng.Fori(first, past, 2) as j:
                step(j, first % 2)
                step(j + 1, (first + 1) % 2)
            for j in range(first + (past - first + 1) // 2 * 2, NTILE + 2):
                step(j, j % 2)

        def row_of(j, first=0, past=C):
            return xg[:, bass.ds(j, 1), first:past].rearrange("p o c -> p (o c)")

        XG_GROUPS = (("xg_in0", 0, 1), ("xg_in1", 1, 3), ("xg_in2", 3, 6), ("xg_in3", 6, NTILE))

        def group_of(j):
            return next(g_ for g_ in XG_GROUPS if g_[1] <= j < g_[2])

        def wait_rows(eng, j):
            if isinstance(j, int):
                for name, first, past in XG_GROUPS:
                    if j == min(first, 5):
                        wait(eng, name, 16 * (past - first))

        def of_parity(j, par, each):
            return (j - par) * (each // 2) + each

        @block.sync
        def _(sp):
            def load(dst, src, name):
                sp.dma_start(dst, src).then_inc(s[name], 16)

            load(xT[:, :], x_cols[0], "xT_in")
            load(wqkv[:, :], wqkv_t, "wqkv_in")
            load(temp[:, :], temperature.partition_broadcast(P), "temp_in")
            load(pbias[:, :], proj_b.partition_broadcast(P), "c_in")
            load(bv_row[:, :], bv.partition_broadcast(P), "c_in")
            load(rb_row[:, :], router_b.partition_broadcast(P), "c_in")
            load(bq_col[:, :], bq.unsqueeze(1), "c_in")
            load(bk_col[:, :], bk.unsqueeze(1), "c_in")
            load(wproj[:, :], wproj_t, "w_in")
            load(wq[:, :], wq_t, "w_in")
            load(wk[:, :], wk_t, "w_in")
            load(wv[:, :], wv_t, "w_in")
            load(wr[:, :], router_w, "w_in")
            load(er[:, :], er_t, "er_in")
            load(brow[:, 0:2 * F], b1, "bias_in")
            load(brow[:, 2 * F:ABIAS], b2, "bias_in")

            def write_parts(dst, Sp, which, rows, name):
                for at, n, first in rows:
                    src = Sp[:, first, which, :].unsqueeze(1).broadcast_to([P, n, NT]) if which else Sp[:, first:first + n, 0, :]
                    load(dst[which, at:at + n].rearrange("w p t -> p w t"), src, name)

            Q_ROWS = ((0, 3, 0), (3, 2, 0), (5, 1, 0))
            K_ROWS = ((0, 3, 0), (3, 2, 1), (5, 1, 2))

            def stack(parts, which):
                return parts[which].rearrange("w (d h) t -> (w d) h t", h=H)

            def of_batch(t_, b):
                return one(t_[bass.ds(b, 1)] if not isinstance(b, int) else t_[b:b + 1])

            def next_x(t, b):
                wait(sp, "ma_full", a_full(t, "qkv1"))
                load(xT[:, :], of_batch(x_cols, (t + 1) % NB), "xT_in")

            def q_k_out(t, b):
                wait(sp, "qs_in", b * 32)
                wait(sp, "spa_ok", b + 1)
                for which, rows in ((0, Q_ROWS), (1, K_ROWS)):
                    write_parts(parts_a, SpA, which, rows, "pa_out")

            def q_k_in(t, b):
                wait(sp, "st_full", b * 16)
                wait(sp, "pa_out", b * 96 + 96)
                for which, st in ((0, QS), (1, KS)):
                    load(st[0:SR, :, :], stack(parts_a, which), "qs_in")

            def shift_rows(t, b):
                wait(sp, "ma_free", a_full(t, "shiftT"))
                sh = of_batch(shift_a, b)
                load(sh.rearrange("q h t -> (q h) t"), nmT[:, :], "m_out")
                wait(sp, "m_out", b * 16 + 16)
                load(QS[96:97, :, :].rearrange("o h (q t) -> o h q t", q=TT), sh.rearrange("q h t -> h q t").unsqueeze(0), "m_in")

            def biases_out(t, b, k):
                if k == 5:
                    wait(sp, "bias_split", 1)
                    load(bias_parts.rearrange("w e f -> e w f"), bparts[:, :, :], "bias_out")

            def context(t, b):
                if not isinstance(b, int) or b > 0:
                    wait(sp, "mb_full", b_full(b - 1, "v"))
                load(cT[:, :], of_batch(ctx_cols, b), "cT_in")
                if isinstance(t, int) and t == 1:
                    wait(sp, "staging_fill", 2)

            def residual_in(t, b):
                wait(sp, "xpb_ok", b)
                load(x_tok[:, :, :], of_batch(x_rows, b), "xtok_in")

            def cross_parts(t, b, which, rows, Zin, ready, done_out, done_in):
                wait(sp, done_in, b * 32)
                wait(sp, ready, b + 1)
                write_parts(parts_b, SpB, which, rows, done_out)
                wait(sp, "z_ok", b * 2)
                wait(sp, done_out, b * 48 + 48)
                for half_ in (0, 64):
                    load(Zin[half_:half_ + SR, :, :], stack(parts_b, which), done_in)

            turns(sp, {
                ("A1", "qkv"): next_x, ("A1", "k"): biases_out, ("A1", "qkT"): q_k_out, ("A1", "qsin"): q_k_in, ("A1", "shT"): shift_rows,
                ("A2", "st"): lambda t, b, u: context(t, b) if u == 0 else None,
                ("A2", "xpb"): residual_in,
                ("A2", "k2T"): lambda t, b: cross_parts(t, b, 1, K_ROWS, KZ, "spk_ok", "pk_out", "kz_in"),
                ("A2", "q2T"): lambda t, b: cross_parts(t, b, 0, Q_ROWS, QZ, "spq_ok", "pq_out", "qz_in"),
            })
            sp.wait_ge(s["st_full"], 16 * NB)
            sp.wait_ge(s["bias_out"], 16)
            for dst, at in ((value_bias, 0), (gate_bias, F)):
                load(dst[0:3, :].rearrange("w (e f) -> w e f", e=E), bias_parts[:, :, at:at + F], "bias_back")
            load(down_bias[0:3, 0:E * C].rearrange("w (e f) -> w e f", e=E), bias_parts[:, :, 2 * F:ABIAS], "bias_back")
            sp.wait_ge(s["row_known"], 1)
            for j in range(NTILE):
                at = sp.value_load(tile_row[0:1, j:j + 1], min_val=0, max_val=E * REGION + (PARKED - 1) * SLOTS)
                if j == 0:
                    sp.wait_ge(s["scat"], scattered(NB))
                load(xg[:, j, :], sorted_x[bass.ds(at, SLOTS), :], group_of(j)[0])

        @block.gpsimd
        def _(pool):
            n = [0]

            def link(ins):
                ins.then_inc(s["pchain"], 1)
                n[0] += 1
                pool.wait_ge(s["pchain"], n[0])

            g = nc.gpsimd
            link(g.memset(half[:, :], -0.5))
            link(g.memset(ident[:, :], 0.0))
            g.affine_select(out=ident[:, :], in_=ident[:, :], compare_op=ALU.not_equal, fill=1.0,
                            base=0, pattern=[[-1, P]], channel_multiplier=1).then_inc(s["ident_ok"], 1)
            pool.wait_ge(s["ident_ok"], 1)
            g.tensor_copy(identb[:, :], ident[:, :]).then_inc(s["consts"], 1)

            def late_constants(t, b):
                if not isinstance(t, int) or t > 0:
                    return
                link(g.memset(blank[:, :], 0.0))
                link(g.iota(blank[:, C:ROW], pattern=[[0, 1]], base=NB * NT, channel_multiplier=1, allow_small_or_imprecise_dtypes=True))
                link(g.memset(before[:, :], 1.0))
                link(g.affine_select(out=before[:, :], in_=before[:, :], compare_op=ALU.is_gt, fill=0.0,
                                     base=0, pattern=[[1, P]], channel_multiplier=-1))
                link(g.iota(x2[:, :, C], pattern=[[P, TT]], base=-NT, channel_multiplier=1, allow_small_or_imprecise_dtypes=True))
                link(g.iota(expert_row[:, :], pattern=[[REGION, E]], base=0, channel_multiplier=0, allow_small_or_imprecise_dtypes=True))
                link(g.iota(iota_e[:, :], pattern=[[1, E]], base=-E, channel_multiplier=0, allow_small_or_imprecise_dtypes=True))
                link(g.iota(iota_t[:, :], pattern=[[1, NTILE]], base=0, channel_multiplier=0, allow_small_or_imprecise_dtypes=True))
                g.iota(iota_c[:, :], pattern=[[SLOTS, NTK]], base=0, channel_multiplier=0, allow_small_or_imprecise_dtypes=True).then_inc(s["consts"], 1)

            def expert_weights(t, b, u):
                if isinstance(t, int) and t == 0 and u < E:
                    if u == 0:
                        pool.wait_ge(s["qs_in"], 32)
                    pool.dma_start(w1_sb[:, u, :], w1[u]).then_inc(s["bigw"], 16)
                if isinstance(t, int) and t == 1 and u < BLANK_PIECES:
                    tiles = sorted_x.rearrange("(j p) c -> p j c", p=P)
                    n_ = -(-tiles.shape[1] // BLANK_PIECES)
                    tiles = tiles[:, u * n_:min((u + 1) * n_, tiles.shape[1]), :]
                    pool.dma_start(tiles, blank[:, :].unsqueeze(1).broadcast_to([P, tiles.shape[1], ROW])).then_inc(s["scat"], 16)
                if isinstance(t, int) and t == 1 and u >= 8:
                    e = u - 8
                    pool.dma_start(w2_sb[:, e, :, :], w2[e].rearrange("(k f) c -> f k c", f=P)).then_inc(s["bigw"], 16)

            def stack_er(t, b, k):
                if k == 0:
                    pool.wait_ge(s["er_split"], 1)
                    for half_, at in ((0, 0), (64, 1)):
                        for blk, w in enumerate((0, 0, 0, 1, 1, 2)):
                            pool.dma_start(ErS[half_ + D * blk:half_ + D * blk + D, at:at + NT], er_parts[:, w, :]).then_inc(s["er_stacked"], 16)
                        pool.dma_start(ErS[half_ + SR:half_ + SR + 1, NT + at:NT + at + 140], er_mask[:, NT:NT + 140]).then_inc(s["er_stacked"], 16)

            def root(dst, src, needs, ready, count):
                wait(pool, needs, count)
                g.tensor_tensor(out=dst, in0=src, in1=half[:, 0:src.shape[1]], op=ALU.pow).then_inc(s[ready], 1)

            def add_bias(t, b):
                wait(pool, "xtok_in", b * 16 + 16)
                pool.wait_ge(s["c_in"], 16 * 5)
                if not isinstance(b, int) or b > 0:
                    wait(pool, "ma_free", a_full(t - 1, "proj"))
                g.tensor_tensor(out=xpb[:, :, :], in0=x_tok[:, :, :],
                                in1=pbias[:, :].unsqueeze(1).broadcast_to([P, TT, C]), op=ALU.add).then_inc(s["xpb_ok"], 1)

            def scatter_rows(t, b):
                wait(pool, "slot_ok", b + 1)
                if not isinstance(b, int):
                    g.tensor_tensor(out=carrier[:, 0:1], in0=half[:, 0:1], in1=half[:, 0:1], op=ALU.add)
                for i in range(TT):
                    pool.indirect_dma_start(out=sorted_x, out_offset=bass.IndirectOffsetOnAxis(ap=slot[:, i:i + 1], axis=0),
                                            in_=x2[:, i, :], in_offset=None).then_inc(s["scat"], 16)

            turns(pool, {
                ("A1", "qkT"): late_constants, ("A1", "d"): expert_weights, ("A1", "k"): stack_er,
                ("A1", "qkn"): lambda t, b: root(rn[:, :], n2c[:, :], "n2c_ok", "rn_ok", b + 1),
                ("A2", "xpb"): add_bias,
                ("A2", "ln"): lambda t, b, _: root(rs1[:, :], ve1[:, :], "ve1_ok", "rs1_ok", b + 1),
                ("B", "ln"): lambda t, b, _: root(rs2[:, :], ve2[:, :], "ve2_ok", "rs2_ok", b + 1),
                ("B", "rk"): scatter_rows,
            })
            def root3(j, par):
                wait(pool, "ve3_ok", j + 1)
                g.tensor_tensor(out=rs3[:, par:par + 1], in0=ve3[:, par:par + 1], in1=half[:, 0:1], op=ALU.pow).then_inc(s["rs3_ok"], 1)

            def rows_home(j, par):
                wait(pool, "x3_ok", j + 1)
                g.tensor_tensor(out=carrier[:, par:par + 1], in0=half[:, 0:1], in1=half[:, 0:1], op=ALU.add)
                pool.indirect_dma_start(out=out.rearrange("b t c -> (b t) c"),
                                        out_offset=bass.IndirectOffsetOnAxis(ap=token[:, par:par + 1], axis=0),
                                        in_=y[:, par, :], in_offset=None, bounds_check=NB * NT - 1, oob_is_err=False)\
                    .then_inc(s[f"o_out{par}"], 16)

            tile_steps(pool, (-1, root3), (-2, rows_home))
            for par in range(2):
                pool.wait_ge(s[f"o_out{par}"], 16 * ((NTILE + 1 - par) // 2))

        @block.scalar
        def _(act):
            a = nc.scalar

            def copy(dst, src):
                return a.activation(dst, src, ACT.Copy)

            def a_out(t, use, dst, src):
                wait(act, "ma_full", a_full(t, use))
                copy(dst, src).then_inc(s["ma_free"], 1)

            def b_out(b, use, dst, src):
                wait(act, "mb_full", b_full(b, use))
                copy(dst, src).then_inc(s["mb_free"], 1)

            def qkv_out(t, b):
                wait(act, "qkn_ok", b)
                for i in range(TT):
                    a_out(t, f"qkv{i}", qkv[:, i, :], MA[:, 0:3 * C])
                wait(act, "ma_free", a_full(t, "qkv1"))
                for i in range(TT):
                    for k in range(2):
                        ins = a.activation(sq[:, 2 * i + k, :], qkv[:, i, k * C:(k + 1) * C], ACT.Square,
                                           accum_out=n2[:, 2 * i + k:2 * i + k + 1])
                ins.then_inc(s["n2_ok"], 1)

            def qkT_out(t, b):
                wait(act, "spa_ok", b)
                a_out(t, "qkT", qkT[:, :, :], MA[:, :].rearrange("p (w t) -> p w t", w=2))

            def values(t, b):
                if isinstance(t, int) and t == 0:
                    wait(act, "v1_fill", 1)
                a.activation(V1[:, :, :, 0:D], qkv[:, :, 2 * C:3 * C].rearrange("p t (h d) -> p t h d", d=D), ACT.Copy)\
                    .then_inc(s["v1_ok"], 1)

            def shifts(t, b):
                wait(act, "m_out", b * 16)
                a_out(t, "shiftT", nmT[:, :], MAb[0:TT * H, 0:P])

            def exp1(t, b, u):
                hp, kt = divmod(u, 2)
                grp, i = divmod(hp, 2)
                wait(act, "st_full", b * 16 + u + 1)
                if u == 8:
                    wait(act, "ma_full", a_full(t, "pv0"))
                a.activation(P1[:, grp % 2, kt, 2 * i:2 * i + 2, :].rearrange("p h t -> p (h t)"),
                             SA[:, kt, :], ACT.Exp).then_inc(s["exp1"], 1)

            def weighed1(t, b, grp):
                if grp % 2:
                    a_out(t, f"pv{grp // 2}", OT1[:, :], MA[:, :])

            def copy_scores(t, b, qb):
                wait(act, "sc_full", b * NQB + qb + 1)
                if qb >= 2:
                    wait(act, "mb_full", b_full(b, f"tr{qb - 2}"))
                if qb >= 6:
                    wait(act, "maxed", b * 4 + qb - 5)
                copy(Sb[:, qb % 2, :], SB[:, 2 * (qb % 2), :]).then_inc(s["copied"], 1)

            def exp2(t, b, qb):
                wait(act, "shifted", b * NQB + qb + 1)
                qs, at = slice(QB * (qb % 4), QB * (qb % 4) + QB), 2 * (qb % 2)
                if qb < 4:
                    a.activation(P2a[:, :, qs], SB[:, at, :].rearrange("p (h q) -> p h q", h=H), ACT.Exp)\
                        .then_inc(s["exp2"], 1)
                else:
                    a.activation(P2b[:, :, :, qs].rearrange("p k h q -> p (k h) q"),
                                 SB[:, at:at + 2, :].rearrange("p k (h q) -> p (k h) q", h=H), ACT.Exp).then_inc(s["exp2"], 1)

            turns(act, {
                ("A1", "qkv"): qkv_out, ("A1", "qkT"): qkT_out, ("A1", "vcp"): values, ("A1", "shT"): shifts,
                ("A2", "st"): exp1, ("A2", "pv"): weighed1,
                ("A2", "oT"): lambda t, b: a_out(t, "oT", O1T[:, :], MA[:, 0:NT]),
                ("A2", "x1T"): lambda t, b: a_out(t, "x1T", x1T[:, :], MA[:, 0:NT]),
                ("B", "sc"): copy_scores, ("B", "sh"): exp2,
                ("B", "pv"): lambda t, b, qt: b_out(b, f"pv{qt}", OT2[:, :], MB[:, :]),
                ("B", "x2T"): lambda t, b: b_out(b, "x2T", x2T[:, :], MB[:, 0:NT]),
            })

            a.activation(early[:, :], early[:, :], ACT.Sigmoid)

            def act_out(j, par):
                wait(act, "down_full", j - 1)
                wait(act, "actT_full", j + 1)
                copy(actT[:, par, :], MB[:, :]).then_inc(s["actT_ok"], 1)

            def gate(j, par):
                wait(act, "act_ok", j - 1)
                wait(act, "gate_full", j + 1)
                a.activation(sg[:, par, :], UP[par][1], ACT.Sigmoid).then_inc(s["sg_ok"], 1)

            def rows_out(j, par):
                wait(act, "up_full", j - 1)
                wait(act, "xgT_full", j + 1)
                copy(xgT[:, par, :], MA[:, 0:P]).then_inc(s["xgT_ok"], 1)

            def stage_row(j, par):
                wait_rows(act, j)
                wait(act, "xgT_full", j - 1)
                copy(row[:, par, :], row_of(j)).then_inc(s["row_ok"], 1)

            tile_steps(act, (-1, act_out), (0, gate), (1, rows_out), (2, stage_row))

        @block.vector
        def _(dve):
            v = nc.vector
            n = [0]
            loop = [0, 0]

            def link(ins):
                ins.then_inc(s["dchain"], 1)
                n[0] += 1
                dve.wait_ge(s["dchain"], loop[0] * loop[1] + n[0])

            def words(tile):
                return tile[:, :, :].rearrange("p h t -> p (h t)").bitcast(U32)

            TWO_ONES = 0x3F803F80

            v.memset(early[:, :], 0.0).then_inc(s["fill"], 1)
            link(v.memset(words(QS), 0))
            link(v.memset(words(KS), 0))
            v.memset(words(KS[96:97, :, :]), TWO_ONES).then_inc(s["fill"], 1)
            dve.wait_ge(s["temp_in"], 16)
            link(v.reciprocal(temp[:, :], temp[:, :]))
            link(v.tensor_scalar(trow[:, :, :], temp[:, :].unsqueeze(1).broadcast_to([P, D, H]), 1.0 / D, None, ALU.mult))

            def value_ones(values_, name):
                link(v.memset(values_[:, :, :, :], 0.0))
                v.memset(values_[:, :, :, D:D + 1], 1.0).then_inc(s[name], 1)

            def split_biases():
                dve.wait_ge(s["bias_in"], 32)
                link(v.tensor_copy(bparts[:, 0, :], brow[:, :]))
                link(v.tensor_tensor(out=brest[:, :], in0=brow[:, :], in1=bparts[:, 0, :], op=ALU.subtract))
                link(v.tensor_copy(bparts[:, 1, :], brest[:, :]))
                v.tensor_tensor(out=bparts[:, 2, :], in0=brest[:, :], in1=bparts[:, 1, :], op=ALU.subtract).then_inc(s["bias_split"], 1)

            def split_er():
                link(v.memset(ErS[:, :].bitcast(U32), 0))
                link(v.memset(er_mask[:, :], MASKED))
                dve.wait_ge(s["er_in"], 16)
                link(v.tensor_copy(er_parts[:, 0, :], er[:, :]))
                link(v.tensor_tensor(out=er_rest[:, :], in0=er[:, :], in1=er_parts[:, 0, :], op=ALU.subtract))
                link(v.tensor_copy(er_parts[:, 1, :], er_rest[:, :]))
                v.tensor_tensor(out=er_parts[:, 2, :], in0=er_rest[:, :], in1=er_parts[:, 1, :], op=ALU.subtract)\
                    .then_inc(s["er_split"], 1)

            def cross_query_rows():
                v.memset(words(QZ), TWO_ONES).then_inc(s["staging_fill"], 1)

            def cross_key_rows():
                v.memset(words(KZ), 0).then_inc(s["staging_fill"], 1)

            def small_constants():
                link(v.memset(parity[:, :], 0.0))
                link(v.memset(parity[0:64, 0:NT:2], 1.0))
                link(v.memset(parity[64:128, 1:NT:2], 1.0))
                link(v.memset(ones_3[:, :], 0.0))
                v.memset(ones_3[0:3, :], 1.0)
                v.memset(ones_b[:, :], 1.0).then_inc(s["fill"], 1)
                dve.wait_ge(s["consts"], 2)
                link(v.memset(cnt[:, :], 0.0))
                for one_ in sums:
                    ins = v.memset(one_[:, :], 0.0)
                link(ins)
                link(v.tensor_copy(start[:, :], expert_row[:, :]))

            def constants(t, b, k):
                (split_er, cross_query_rows, cross_key_rows, small_constants, lambda: value_ones(V2, "fill"), split_biases)[k]()

            def split(parts, which, whole, rest, ready):
                p = [parts[:, k, which, :] for k in range(3)]
                link(v.tensor_copy(p[0], whole))
                link(v.tensor_tensor(out=rest, in0=whole, in1=p[0], op=ALU.subtract))
                link(v.tensor_copy(p[1], rest))
                v.tensor_tensor(out=p[2], in0=rest, in1=p[1], op=ALU.subtract).then_inc(s[ready], 1)

            def layer_norm(b, r, st, mv, ve, rs, dst, ntiles, ve_ok, rs_ok, done):
                for t in range(ntiles):
                    link(v.bn_stats(st[:, t, :], r[:, t, :]))
                v.memset(pad[:, :], 0.0)
                for t in range(ntiles):
                    ins = v.bn_aggr(mv[:, t, :], st[:, t, :])
                link(ins)
                v.tensor_scalar(ve[:, :], mv[:, :, 1], LN_EPS, None, ALU.add).then_inc(s[ve_ok], 1)
                wait(dve, rs_ok, b + 1)
                for t in range(ntiles):
                    ins = v.tensor_scalar(dst[:, t, 0:C], r[:, t, :], mv[:, t, 0:1], rs[:, t:t + 1], ALU.subtract, ALU.mult)
                ins.then_inc(s[done], 1)

            def normalise(box, rden, dst):
                link(v.reciprocal(rden, box[:, :, :, D]))
                return v.tensor_tensor(out=dst, in0=box[:, :, :, 0:D],
                                       in1=rden.unsqueeze(3).broadcast_to([P, box.shape[1], box.shape[2], D]), op=ALU.mult)

            def clamp_norms(t, b):
                wait(dve, "n2_ok", b + 1)
                v.tensor_scalar(n2c[:, :], n2[:, :], 1e-24, None, ALU.max).then_inc(s["n2c_ok"], 1)
                if isinstance(t, int) and t == 0:
                    value_ones(V1, "v1_fill")

            def scale_q_k(t, b):
                wait(dve, "rn_ok", b + 1)
                for i in range(TT):
                    v.scalar_tensor_tensor(out=qkn[:, i, 0, :, :].rearrange("p d h -> p h d"),
                                           in0=qkv[:, i, 0:C].rearrange("p (h d) -> p h d", d=D),
                                           scalar=rn[:, 2 * i:2 * i + 1],
                                           in1=trow[:, :, :].rearrange("p d h -> p h d"), op0=ALU.mult, op1=ALU.mult)
                    ins = v.tensor_scalar(qkn[:, i, 1, :, :].rearrange("p d h -> p h d"),
                                          qkv[:, i, C:2 * C].rearrange("p (h d) -> p h d", d=D),
                                          rn[:, 2 * i + 1:2 * i + 2], None, ALU.mult)
                ins.then_inc(s["qkn_ok"], 1)

            def split_q_k(t, b):
                wait(dve, "ma_free", a_full(t, "qkT"))
                wait(dve, "pa_out", b * 96)
                p = [SpA[:, k, :, :] for k in range(3)]
                link(v.tensor_copy(p[0], qkT[:, :, :]))
                link(v.tensor_tensor(out=restA[:, :, :], in0=qkT[:, :, :], in1=p[0], op=ALU.subtract))
                link(v.tensor_copy(p[1], restA[:, :, :]))
                v.tensor_tensor(out=p[2], in0=restA[:, :, :], in1=p[1], op=ALU.subtract).then_inc(s["spa_ok"], 1)

            def maxima(t, b, u):
                hp, qt = divmod(u, 2)
                wait(dve, "sa_full", b * 16 + u + 1)
                v.tensor_reduce(out=negm1[:, qt, 2 * hp:2 * hp + 2], in_=SA[:, u % 2, :].rearrange("p (h k) -> p h k", h=2),
                                axis=AX.X, op=ALU.max, negate=True).then_inc(s["negm1_ok"], 1)

            def norm1(t, b, pair):
                wait(dve, "ma_full", a_full(t, f"norm{pair}"))
                normalise(MA[:, :].rearrange("p (q h w) -> p q h w", q=TT, w=VW), rden1[:, :, :],
                          O1[:, :, 64 * pair:64 * pair + 64].rearrange("p q (h d) -> p q h d", d=D)).then_inc(s["ma_free"], 1)

            def residual1(t, b):
                wait(dve, "ma_full", a_full(t, "proj"))
                wait(dve, "xpb_ok", b + 1)
                v.tensor_tensor(out=res1[:, :, :], in0=MA[:, 0:NT].rearrange("p (t c) -> p t c", t=TT), in1=xpb[:, :, :],
                                op=ALU.add).then_inc(s["ma_free"], 1)

            def ln1(t, b, _):
                wait(dve, "ma_free", a_full(t, "proj"))
                layer_norm(b, res1, st1, mv1, ve1, rs1, x1, TT, "ve1_ok", "rs1_ok", "x1_ok")

            def keys2(t, b):
                wait(dve, "ma_full", a_full(t, "k2T"))
                v.tensor_scalar(qk2T[:, 1, :], MA[:, 0:NT], bk_col[:, :], None, ALU.add).then_inc(s["ma_free"], 1)
                wait(dve, "ma_free", a_full(t, "k2T"))
                split(SpB, 1, qk2T[:, 1, :], restB[:, 1, :], "spk_ok")

            def queries2(t, b):
                wait(dve, "ma_full", a_full(t, "q2T"))
                v.tensor_scalar(qk2T[:, 0, :], MA[:, 0:NT], bq_col[:, :], float(D) ** -0.5, ALU.add, ALU.mult)\
                    .then_inc(s["ma_free"], 1)
                wait(dve, "ma_free", a_full(t, "q2T"))
                split(SpB, 0, qk2T[:, 0, :], restB[:, 0, :], "spq_ok")

            def values2(t, b):
                wait(dve, "mb_full", b_full(b, "v"))
                v.tensor_tensor(out=V2[:, :, :, 0:D], in0=MB[:, 0:NT].rearrange("p (t h d) -> p t h d", t=TT, d=D),
                                in1=bv_row[:, :].rearrange("p (h d) -> p h d", d=D).unsqueeze(1).broadcast_to([P, TT, H, D]),
                                op=ALU.add).then_inc(s["mb_free"], 1)

            def copy_keys(t, b):
                wait(dve, "sc_full", b * NQB)
                wait(dve, "kz_in", b * 32 + 32)
                v.tensor_copy(KS2[:, :, :], KZ[:, :, :])

            def even_odd(b, part):
                q = slice(part * P, (part + 1) * P)
                v.tensor_tensor(out=Z[:, :, q], in0=QZ[:, :, q], in1=parity[:, q].unsqueeze(1).broadcast_to([P, H, P]),
                                op=ALU.mult).then_inc(s["z_ok"], 1)

            def stacks2(t, b):
                wait(dve, "x1_ok", b + 1)
                v.tensor_copy(x1k[:, :, :], x1[:, :, :])
                wait(dve, "qz_in", b * 32 + 32)
                even_odd(b, 0)

            def stacks2_rest(t, b):
                even_odd(b, 1)

            def max_tiles(t, b, qb):
                if qb >= 4:
                    wait(dve, "copied", b * NQB + qb + 1)
                    v.tensor_tensor(out=Sm[:, qb % 2, :], in0=SB[:, 2 * (qb % 2) + 1, :], in1=Sb[:, qb % 2, :],
                                    op=ALU.max).then_inc(s["maxed"], 1)

            def maxima2(t, b, qb):
                wait(dve, "mb_full", b_full(b, f"tr{qb}"))
                v.tensor_reduce(out=negm2[:, qb, :], in_=MBb[:, 0:512].rearrange("p (c k) -> p c k", c=4), axis=AX.X,
                                op=ALU.max, negate=True).then_inc(s["mb_free"], 1)

            def norm2(t, b, qt):
                wait(dve, "mb_full", b_full(b, f"norm{qt}"))
                normalise(MB[:, :].rearrange("p (o h w) -> p o h w", o=1, w=VW), rden2[:, :].unsqueeze(1),
                          O2[:, qt, :].rearrange("p (o h d) -> p o h d", o=1, d=D)).then_inc(s["mb_free"], 1)

            def ln2(t, b, _):
                wait(dve, "mb_free", b_full(b, "norm1") + 1)
                link(v.tensor_tensor(out=res2[:, :, :], in0=O2[:, :, :], in1=x1k[:, :, :], op=ALU.add))
                wait(dve, "scat", scattered(b))
                link(v.tensor_scalar(x2[:, :, C], x2[:, :, C], float(NT), None, ALU.add))
                layer_norm(b, res2, st2, mv2, ve2, rs2, x2, TT, "ve2_ok", "rs2_ok", "x2_ok")

            def bc(ap, axis, shape):
                return ap.unsqueeze(axis).broadcast_to(shape)

            TE = [P, TT, E]

            def choose(t, b):
                wait(dve, "mb_full", b_full(b, "logits"))
                v.tensor_tensor(out=logits[:, :, :], in0=MB[:, 0:TT * E].rearrange("p (t e) -> p t e", t=TT),
                                in1=bc(rb_row[:, :], 1, TE), op=ALU.add).then_inc(s["mb_free"], 1)
                wait(dve, "mb_free", b_full(b, "logits") + 1)
                link(v.tensor_reduce(out=mx[:, :], in_=logits[:, :, :], axis=AX.X, op=ALU.max))
                link(v.tensor_tensor(out=eq[:, :, :], in0=logits[:, :, :], in1=bc(mx[:, :], 2, TE), op=ALU.is_ge))
                link(v.tensor_tensor(out=cand[:, :, :], in0=eq[:, :, :], in1=bc(iota_e[:, :], 1, TE), op=ALU.mult))
                link(v.tensor_reduce(out=first[:, :], in_=cand[:, :, :], axis=AX.X, op=ALU.min))
                link(v.tensor_tensor(out=oh[:, :, :], in0=bc(iota_e[:, :], 1, TE), in1=bc(first[:, :], 2, TE), op=ALU.is_equal))
                v.tensor_copy(ohb[:, :, :], oh[:, :, :]).then_inc(s["oh_ok"], 1)

            def place(t, b):
                wait(dve, "mb_full", b_full(b, "ranks"))
                link(v.tensor_tensor(out=pos[:, :, :], in0=MB[:, 0:TT * E].rearrange("p (t e) -> p t e", e=E), in1=bc(start[:, :], 1, TE), op=ALU.add))
                link(v.tensor_tensor(out=mine[:, :, :], in0=pos[:, :, :], in1=oh[:, :, :], op=ALU.mult))
                link(v.tensor_reduce(out=slotf[:, :], in_=mine[:, :, :], axis=AX.X, op=ALU.add))
                v.tensor_copy(slot[:, :], slotf[:, :]).then_inc(s["slot_ok"], 1)
                link(v.tensor_tensor(out=start[:, :], in0=MB[:, TT * E:(TT + 1) * E], in1=start[:, :], op=ALU.add))
                v.tensor_tensor(out=cnt[:, :], in0=MB[:, TT * E:(TT + 1) * E], in1=cnt[:, :], op=ALU.add).then_inc(s["mb_free"], 1)
                wait(dve, "mb_free", b_full(b, "ranks") + 1)

            before_loop = [0]

            def looped(t):
                if t is not None:
                    before_loop[0] = n[0]
                    loop[:] = [t - FIRST_FULL, LINKS_A_TURN]
                else:
                    assert n[0] - before_loop[0] == LINKS_A_TURN, n[0] - before_loop[0]
                    loop[:] = [0, 0]
                    n[0] = before_loop[0] + (PAST_FULL - FIRST_FULL) * LINKS_A_TURN

            dve.sem_inc(s["mb_free"], 1)
            dve.wait_ge(s["c_in"], 16 * 5)
            turns(dve, {
                ("A1", "qkv"): clamp_norms, ("A1", "qkn"): scale_q_k, ("A1", "qkT"): split_q_k, ("A1", "d"): maxima, ("A1", "k"): constants,
                ("A2", "nm"): norm1, ("A2", "proj"): residual1, ("A2", "ln"): ln1, ("A2", "k2T"): keys2, ("A2", "q2T"): queries2,
                ("B", "v"): values2, ("B", "build"): stacks2, ("B", "rest"): stacks2_rest, ("A2", "kc"): copy_keys, ("B", "sc"): max_tiles, ("B", "tr"): maxima2, ("B", "nm"): norm2,
                ("B", "ln"): ln2, ("B", "lg"): choose, ("B", "rk"): place,
            }, looped)

            link(v.tensor_tensor(out=gt[:, :, :], in0=bc(cnt[:, :], 2, [P, E, NTK]), in1=bc(iota_c[:, :], 1, [P, E, NTK]), op=ALU.is_gt))
            link(v.tensor_reduce(out=nti[:, :], in_=gt[:, :, :], axis=AX.X, op=ALU.add))
            for k, back in enumerate((1, 2, 4)):
                link(v.tensor_tensor(out=sums[k + 1][:, E // 2:], in0=sums[k][:, E // 2:], in1=sums[k][:, E // 2 - back:E // 2 - back + E], op=ALU.add))
            link(v.tensor_tensor(out=le[:, :, :], in0=bc(ends[:, :], 1, [P, NTILE, E]), in1=bc(iota_t[:, :], 2, [P, NTILE, E]), op=ALU.is_le))
            link(v.tensor_scalar(skip[:, :], nti[:, :], -float(SLOTS), float(REGION), ALU.mult, ALU.add))
            link(v.tensor_tensor(out=skips[:, :, :], in0=le[:, :, :], in1=bc(skip[:, :], 1, [P, NTILE, E]), op=ALU.mult))
            link(v.tensor_reduce(out=skipped[:, :], in_=skips[:, :, :], axis=AX.X, op=ALU.add))
            v.scalar_tensor_tensor(out=tile_row[:, :], in0=iota_t[:, :], scalar=float(SLOTS), in1=skipped[:, :],
                                   op0=ALU.mult, op1=ALU.add).then_inc(s["row_known"], 1)
            link(v.tensor_reduce(out=tef[:, :], in_=le[:, :, :], axis=AX.X, op=ALU.add))
            v.tensor_scalar(tile_e[:, :], tef[:, :], float(E - 1), None, ALU.min).then_inc(s["te_ok"], 1)

            def glu(j, par):
                wait(dve, "actT_full", j - 1)
                wait(dve, "up_full", j + 1)
                wait(dve, "sg_ok", j + 1)
                v.tensor_tensor(out=act_[:, par, :], in0=UP[par][0], in1=sg[:, par, :], op=ALU.mult).then_inc(s["act_ok"], 1)

            def residual3(j, par):
                wait(dve, "x3_ok", j - 1)
                if isinstance(j, int) and j <= 2:
                    for tile in (j,) if j < 2 else range(2, 6):
                        wait_rows(dve, tile)
                wait(dve, "down_full", j + 1)
                v.tensor_tensor(out=res3[:, par, :], in0=SB[:, 2 + par, 0:C], in1=row_of(j), op=ALU.add).then_inc(s["res3_ok"], 1)
                wait(dve, "res3_ok", j + 1)
                v.bn_stats(st3[:, par, :], res3[:, par, :]).then_inc(s["st3_ok"], 1)
                wait(dve, "st3_ok", j + 1)
                v.memset(pad[:, :], 0.0)
                v.bn_aggr(mv3[:, par, :], st3[:, par, :]).then_inc(s["mv3_ok"], 1)
                wait(dve, "mv3_ok", j + 1)
                v.tensor_scalar(ve3[:, par:par + 1], mv3[:, par, 1:2], LN_EPS, None, ALU.add).then_inc(s["ve3_ok"], 1)

            def norm3(j, par):
                wait(dve, f"o_out{par}", of_parity(j, par, 16) - 16)
                wait(dve, "rs3_ok", j + 1)
                v.tensor_copy(token[:, par:par + 1], row_of(j, C, ROW))
                v.tensor_scalar(y[:, par, :], res3[:, par, :], mv3[:, par, 0:1], rs3[:, par:par + 1], ALU.subtract, ALU.mult)\
                    .then_inc(s["x3_ok"], 1)

            tile_steps(dve, (0, glu), (-1, residual3), (-2, norm3))

        @block.tensor
        def _(pe):
            mm = nc.tensor.matmul

            def tr(dst, src, idn):
                return nc.tensor.transpose(dst, src, idn)

            def a_box(t, use):
                wait(pe, "ma_free", a_full(t, use) - 1)

            def b_box(b, use):
                wait(pe, "mb_free", b_full(b, use))

            def project_x(t, b):
                wait(pe, "xT_in", b * 16 + 16)
                for i in range(TT):
                    a_box(t, f"qkv{i}")
                    mm(MA[:, 0:3 * C], xT[:, i * P:(i + 1) * P], wqkv[:, :], start=True, stop=True).then_inc(s["ma_full"], 1)

            def transpose_q_k(t, b):
                wait(pe, "qkn_ok", b + 1)
                a_box(t, "qkT")
                for w in range(2):
                    for i in range(TT):
                        last = tr(MA[:, w * NT + i * P:w * NT + (i + 1) * P], qkn[:, i, w, :, :].rearrange("p d h -> p (d h)"), ident[:, :])
                last.then_inc(s["ma_full"], 1)

            def scores1(t, b, u):
                hp, qt = divmod(u, 2)
                if u == 0:
                    wait(pe, "qs_in", b * 32 + 32)
                if u < 2:
                    wait(pe, "exp1", b * 16)
                else:
                    wait(pe, "negm1_ok", b * 16 + u - 1)
                for i in range(2):
                    h = 2 * hp + i
                    last = mm(SA[:, u % 2, i * NT:(i + 1) * NT], QS[0:96, h, qt * P:(qt + 1) * P], KS[0:96, h, :], start=True, stop=True)
                last.then_inc(s["sa_full"], 1)

            def transpose_shifts(t, b):
                cross_constants(t, b)
                wait(pe, "negm1_ok", b * 16 + 16)
                a_box(t, "shiftT")
                tr(MAb[0:TT * H, 0:P], negm1[:, :, :].rearrange("p q h -> p (q h)"), identb[:, :]).then_inc(s["ma_full"], 1)

            def scores_t(t, b, u):
                hp, kt = divmod(u, 2)
                if u == 0:
                    wait(pe, "m_in", b * 16 + 16)
                    wait(pe, "negm1_ok", b * 16 + 16)
                elif u >= 2:
                    wait(pe, "exp1", b * 16 + u - 1)
                for i in range(2):
                    h = 2 * hp + i
                    last = mm(SA[:, kt, i * NT:(i + 1) * NT], KS[:, h, kt * P:(kt + 1) * P], QS[:, h, :], start=True, stop=True)
                last.then_inc(s["st_full"], 1)

            def weigh1(t, b, grp):
                if grp == 0:
                    wait(pe, "v1_ok", b + 1)
                wait(pe, "exp1", b * 16 + 4 * grp + 4)
                if grp % 2 == 0:
                    a_box(t, f"pv{grp // 2}")
                for kt in range(TT):
                    for i in range(HEADS_A_GROUP):
                        h = grp * HEADS_A_GROUP + i
                        last = mm(MA[VW * i:VW * i + VW, (grp % 2) * NT:(grp % 2 + 1) * NT], V1[:, kt, h, :],
                                  P1[:, grp % 2, kt, i, :], start=(kt == 0), stop=(kt == TT - 1))
                if grp % 2:
                    last.then_inc(s["ma_full"], 1)

            def transpose_o(t, b, pair):
                a_box(t, f"norm{pair}")
                for qt in range(TT):
                    for g2 in range(2):
                        last = tr(MA[:, qt * 256 + g2 * P:qt * 256 + (g2 + 1) * P],
                                  OT1[:, g2 * NT + qt * P:g2 * NT + (qt + 1) * P], ident[:, :])
                last.then_inc(s["ma_full"], 1)

            def transpose_rows(src):
                for i in range(TT):
                    last = tr(MA[:, i * P:(i + 1) * P], src[:, i, :], ident[:, :])
                return last

            def o_to_cols(t, b):
                a_box(t, "oT")
                transpose_rows(O1).then_inc(s["ma_full"], 1)

            def project_o(t, b):
                a_box(t, "proj")
                for i in range(TT):
                    last = mm(MA[:, i * C:(i + 1) * C], O1T[:, i * P:(i + 1) * P], wproj[:, :], start=True, stop=True)
                last.then_inc(s["ma_full"], 1)

            def x1_to_cols(t, b):
                wait(pe, "x1_ok", b + 1)
                a_box(t, "x1T")
                transpose_rows(x1).then_inc(s["ma_full"], 1)

            def project_q2(t, b):
                a_box(t, "q2T")
                mm(MA[:, 0:NT], wq[:, :], x1T[:, :], start=True, stop=True).then_inc(s["ma_full"], 1)

            def project_k2(t, b):
                wait(pe, "cT_in", b * 16 + 16)
                a_box(t, "k2T")
                mm(MA[:, 0:NT], wk[:, :], cT[:, :], start=True, stop=True).then_inc(s["ma_full"], 1)

            def project_v2(t, b):
                b_box(b, "v")
                for i in range(TT):
                    last = mm(MB[:, i * C:(i + 1) * C], cT[:, i * P:(i + 1) * P], wv[:, :], start=True, stop=True)
                last.then_inc(s["mb_full"], 1)

            def scores2(t, b, qb):
                if qb in (0, 4):
                    wait(pe, "z_ok", b * 2 + 1 + qb // 4)
                if qb >= 2:
                    wait(pe, "exp2", b * NQB + qb - 1)
                for kt in range(1 if qb < 4 else 2):
                    bank = SB[:, 2 * (qb % 2) + kt, :].rearrange("p (h q) -> p h q", h=H)
                    for h in range(H):
                        mm(bank[:, h, :], KS2[:, h, kt * P:(kt + 1) * P], Z[:, h, QB * qb:QB * (qb + 1)],
                           start=(h == 0), stop=False, skip_group_check=True)
                    for q in range(0, QB, 2):
                        w = NT - 1 - (QB * qb + q) + kt * P
                        last = mm(bank[:, :, q:q + 2], ErS[:, w:w + P], Z[:, :, QB * qb + q:QB * qb + q + 2],
                                  start=False, stop=False, skip_group_check=True)
                last.then_inc(s["sc_full"], 1)

            def transpose_scores(t, b, qb):
                if qb < 4:
                    wait(pe, "copied", b * NQB + qb + 1)
                else:
                    wait(pe, "maxed", b * 4 + qb - 3)
                src = Sb if qb < 4 else Sm
                b_box(b, f"tr{qb}")
                for c in range(4):
                    last = tr(MBb[:, c * P:(c + 1) * P], src[:, qb % 2, c * P:(c + 1) * P], identb[:, :])
                last.then_inc(s["mb_full"], 1)

            def shift(t, b, qb):
                wait(pe, "mb_free", b_full(b, f"tr{qb}") + 1)
                for kt in range(1 if qb < 4 else 2):
                    for c in range(4):
                        last = mm(SB[:, 2 * (qb % 2) + kt, c * P:(c + 1) * P], negm2[:, qb, c:c + 1].broadcast_to([P, P]),
                                  identb[:, :], start=False, stop=True, skip_group_check=True)
                last.then_inc(s["shifted"], 1)

            def weigh2(t, b, qt):
                wait(pe, "exp2", b * NQB + 4 * qt + 4)
                b_box(b, f"pv{qt}")
                for grp in range(NG):
                    for kt in range(qt + 1):
                        for i in range(HEADS_A_GROUP):
                            h = grp * HEADS_A_GROUP + i
                            rhs = P2a[:, h, :] if qt == 0 else P2b[:, kt, h, :]
                            last = mm(MB[VW * i:VW * i + VW, grp * P:(grp + 1) * P], V2[:, kt, h, :], rhs,
                                      start=(kt == 0), stop=(kt == qt))
                last.then_inc(s["mb_full"], 1)

            def transpose_o2(t, b, qt):
                b_box(b, f"norm{qt}")
                for grp in range(NG):
                    last = tr(MB[:, grp * P:(grp + 1) * P], OT2[:, grp * P:(grp + 1) * P], ident[:, :])
                last.then_inc(s["mb_full"], 1)

            def x2_to_cols(t, b):
                wait(pe, "x2_ok", b + 1)
                b_box(b, "x2T")
                for i in range(TT):
                    last = tr(MB[:, i * P:(i + 1) * P], x2[:, i, 0:C], ident[:, :])
                last.then_inc(s["mb_full"], 1)

            def router(t, b):
                b_box(b, "logits")
                for i in range(TT):
                    last = mm(MB[:, i * E:(i + 1) * E], x2T[:, i * P:(i + 1) * P], wr[:, :], start=True, stop=True)
                last.then_inc(s["mb_full"], 1)

            pe.wait_ge(s["ident_ok"], 1)
            pe.wait_ge(s["consts"], 1)
            pe.wait_ge(s["wqkv_in"], 16)

            def rank(t, b):
                wait(pe, "oh_ok", b + 1)
                b_box(b, "ranks")
                mm(MB[:, 0:TT * E], before[:, :], ohb[:, :, :].rearrange("p t e -> p (t e)"), start=True, stop=False, skip_group_check=True)
                mm(MB[:, E:2 * E], ones_b[:, :], ohb[:, 0, :], start=False, stop=False, skip_group_check=True)
                for i in range(TT):
                    last = mm(MB[:, TT * E:(TT + 1) * E], ones_b[:, :], ohb[:, i, :], start=False, stop=(i == TT - 1), skip_group_check=True)
                last.then_inc(s["mb_full"], 1)

            def cross_constants(t, b):
                if isinstance(t, int) and t == 1:
                    pe.wait_ge(s["fill"], 4)
                    pe.wait_ge(s["staging_fill"], 2)
                    pe.wait_ge(s["er_stacked"], 16 * 14)

            def first_weights(t, b):
                if isinstance(t, int) and t == 0:
                    pe.wait_ge(s["w_in"], 16 * 5)
                    pe.wait_ge(s["fill"], 2)

            turns(pe, {
                ("A1", "qkv"): project_x, ("A1", "qkT"): transpose_q_k, ("A1", "d"): scores1, ("A1", "shT"): transpose_shifts,
                ("A1", "vcp"): first_weights, ("A2", "q2T"): project_q2,
                ("A2", "st"): scores_t, ("A2", "pv"): weigh1, ("A2", "nm"): transpose_o, ("A2", "oT"): o_to_cols,
                ("A2", "proj"): project_o, ("A2", "x1T"): x1_to_cols, ("A2", "k2T"): project_k2,
                ("B", "v"): project_v2, ("B", "sc"): scores2, ("B", "tr"): transpose_scores, ("B", "sh"): shift,
                ("B", "pv"): weigh2, ("B", "nm"): transpose_o2, ("B", "x2T"): x2_to_cols, ("B", "lg"): router,
                ("B", "rk"): rank,
            })
            last_use = fills(A_FILLS, TURNS - 2)[-1]
            pe.wait_ge(s["ma_free"], a_full(TURNS - 2, last_use))
            for _ in range(WARMING):
                mm(MA[:, :], identb[:, :], Z[:, 0:2, :].rearrange("p h t -> p (h t)"), start=True, stop=True)
            pe.wait_ge(s["te_ok"], 1)
            pe.wait_ge(s["bigw"], 16 * 2 * E)
            pe.wait_ge(s["bias_back"], 16 * 3)

            expert = {}

            def read_up(j, par):
                expert["up"] = pe.value_load(tile_e[0:1, bass.ds(j, 1)], min_val=0, max_val=E - 1)

            def read_down(j, par):
                expert["down"] = pe.value_load(tile_e[0:1, bass.ds(j, 1)], min_val=0, max_val=E - 1)

            def rows_to_cols(j, par):
                wait(pe, "xgT_ok", j)
                wait(pe, "row_ok", j + 1)
                tr(MA[:, 0:P], row[:, par, :], ident[:, :]).then_inc(s["xgT_full"], 1)

            def up(j, par):
                e = expert["up"]
                wait(pe, "act_ok", j - 1)
                wait(pe, "xgT_ok", j + 1)
                for k, bias, full in ((1, gate_bias, "gate_full"), (0, value_bias, "up_full")):
                    mm(UP[par][k], ones_3[:, :], bias[:, bass.ds(e * F, F)], start=True, stop=False)
                    mm(UP[par][k], xgT[:, par, :], w1_sb[:, bass.ds(e, 1), k * F:(k + 1) * F].rearrange("p o f -> p (o f)"),
                       start=False, stop=True).then_inc(s[full], 1)

            def transpose_act(j, par):
                wait(pe, "actT_ok", j)
                wait(pe, "act_ok", j + 1)
                for k in range(F // P):
                    last = tr(MB[:, k * P:(k + 1) * P], act_[:, par, k * P:(k + 1) * P], ident[:, :])
                last.then_inc(s["actT_full"], 1)

            def down(j, par):
                e = expert["down"]
                wait(pe, "res3_ok", j - 1)
                wait(pe, "actT_ok", j + 1)
                mm(SB[:, 2 + par, 0:C], ones_3[:, :], down_bias[:, bass.ds(e * C, C)], start=True, stop=False)
                for k in range(F // P):
                    last = mm(SB[:, 2 + par, 0:C], actT[:, par, k * P:(k + 1) * P],
                              w2_sb[:, bass.ds(e, 1), k, :].rearrange("p o c -> p (o c)"), start=False, stop=(k == F // P - 1))
                last.then_inc(s["down_full"], 1)

            tile_steps(pe, (0, read_up), (-1, read_down), (-1, transpose_act), (0, up), (1, rows_to_cols), (-1, down))


def kernel(**inputs):
    import numpy as np
    import concourse.bacc as bacc
    from concourse.bass_utils import run_bass_kernel_spmd as run

    def cols(a):
        return np.asarray(a).transpose(0, 2, 1)

    def by_part(w):
        w = np.asarray(w)
        return w.reshape((H, D) + w.shape[1:]).swapaxes(0, 1).reshape(w.shape)

    i = {k: np.asarray(v) for k, v in inputs.items()}
    arrays = {
        "x_rows": i["x"].reshape(NB, TT, P, C).transpose(0, 2, 1, 3),
        "x_cols": cols(i["x"]),
        "ctx_cols": cols(i["ctx_1024"]),
        "wqkv_t": i["L0_attn_qkv_w"].T,
        "temperature": i["L0_attn_temperature"].reshape(H),
        "wproj_t": i["L0_attn_proj_w"].T,
        "proj_b": i["L0_attn_proj_b"],
        "wq_t": by_part(i["L0_xattn_Wq"]).T,
        "bq": by_part(i["L0_xattn_bq"]),
        "wk_t": by_part(i["L0_xattn_Wk"]).T,
        "bk": by_part(i["L0_xattn_bk"]),
        "wv_t": i["L0_xattn_Wv"].T,
        "bv": i["L0_xattn_bv"],
        "er_t": i["L0_xattn_Er"].T,
        "router_w": i["L0_ffn_router_w"],
        "router_b": i["L0_ffn_router_b"],
        "w1": i["L0_ffn_w1"],
        "b1": i["L0_ffn_b1"],
        "w2": i["L0_ffn_w2"],
        "b2": i["L0_ffn_b2"],
    }
    arrays = {k: np.ascontiguousarray(v) for k, v in arrays.items()}
    nc = bacc.Bacc("TRN2", target_bir_lowering=False, num_devices=1)
    args = [nc.dram_tensor("in_" + k, a.shape, FP32, kind="ExternalInput").ap() for k, a in arrays.items()]
    out = nc.dram_tensor("out", (NB, NT, C), FP32, kind="ExternalOutput").ap()
    build(nc, *args, out)
    r = run(nc, [{"in_" + k: a for k, a in arrays.items()}], core_ids=[0])
    return r.results[0]["out"]
```
